# Optimizing a Trainium2 kernel written in Bass

```python
import numpy as np
import jax
import jax.numpy as jnp

def _softmax(x, axis=-1):
    return jax.nn.softmax(x, axis=axis)

def _gelu(x):
    return jax.nn.gelu(x, approximate=True)

def _silu(x):
    return jax.nn.silu(x)

def _sigmoid(x):
    return jax.nn.sigmoid(x)

def _layernorm(x, axis=-1, eps=1e-05):
    m = jnp.mean(x, axis=axis, keepdims=True)
    v = jnp.var(x, axis=axis, keepdims=True)
    return (x - m) / jnp.sqrt(v + eps)

def _scatter_add(tgt, idx, src, axis=0):
    return tgt.at[idx].add(src)

def _segment_sum(src, seg, n):
    return jax.ops.segment_sum(src, seg, n)
kernel_name = 'mk_gnn_preln_d2_gnn_r8_f298a7'

def setup_inputs(seed: int=0):
    np.random.seed(seed)
    _w = jnp.asarray

    def _rec_inputs():
        import jax
        import jax.numpy as jnp
        _gk = jax.random.key(seed)
        x = -0.000202 + 1 * jax.random.normal(jax.random.fold_in(_gk, 1), (12500, 128), jnp.float32)
        src = jax.random.randint(jax.random.fold_in(_gk, 2), (400000,), 0, 12500, jnp.int32)
        dst = jnp.minimum((12500 * jax.random.uniform(jax.random.fold_in(_gk, 3), (400000,)) ** 2.0).astype(jnp.int32), 99999)
        _o = jnp.argsort(dst, stable=True)
        src = src[_o]
        dst = dst[_o]
        edge_attr_32 = -5.3897e-05 + 0.999841 * jax.random.normal(jax.random.fold_in(_gk, 11), (400000, 32), jnp.float32)
        return (x, src, dst, edge_attr_32)
    x, src, dst, edge_attr_32 = _rec_inputs()

    def _L0_gnn_setup():
        import jax, jax.numpy as jnp
        import numpy as np
        BN_EPS = 1e-05
        key = jax.random.key(seed)
        ks = jax.random.split(key, 16)
        N, E = (6250, 100000)
        IN, OUT, EA, EE = (128, 128, 32, 16)
        s = lambda k, fi, fo: jax.random.normal(k, (fi, fo), jnp.float32) / np.sqrt(fi)
        return {'x': jax.random.normal(ks[0], (N, IN), jnp.float32), 'edge_attr': jax.random.normal(ks[1], (E, EA), jnp.float32), 'W_emb': s(ks[2], EA, EE), 'b_emb': jnp.zeros((EE,), jnp.float32), 'W_temb': s(ks[3], EE, OUT), 'b_temb': jnp.zeros((OUT,), jnp.float32), 'W_tattr': s(ks[4], EA, OUT), 'b_tattr': jnp.zeros((OUT,), jnp.float32), 'W_gate': s(ks[5], 3 * OUT, OUT), 'b_gate': jnp.zeros((OUT,), jnp.float32), 'W_l': s(ks[6], IN, OUT), 'b_l': jnp.zeros((OUT,), jnp.float32), 'W_r': s(ks[7], IN, OUT), 'gamma': jnp.ones((OUT,), jnp.float32), 'beta': jnp.zeros((OUT,), jnp.float32), 'edge_index': jax.random.randint(ks[8], (2, E), 0, N, jnp.int64 if jax.config.jax_enable_x64 else jnp.int32)}
    _L0_gnn_all = _L0_gnn_setup()
    _L0_gnn_in = {k: v for k, v in _L0_gnn_all.items() if k in ('W_emb', 'b_emb', 'W_temb', 'b_temb', 'W_tattr', 'b_tattr', 'W_gate', 'b_gate', 'W_l', 'b_l', 'W_r', 'gamma', 'beta')}
    del _L0_gnn_all

    def _L1_gnn_setup():
        import jax, jax.numpy as jnp
        import numpy as np
        N_NODES = 12500
        N_EDGES = 200000
        IN_DIM, HID_DIM, OUT_DIM = (128, 64, 128)

        def gcn_conv(x, edge_index, W, b):
            n = x.shape[0]
            loop = jnp.arange(n, dtype=edge_index.dtype)
            src = jnp.concatenate([edge_index[0], loop])
            dst = jnp.concatenate([edge_index[1], loop])
            deg = jax.ops.segment_sum(jnp.ones_like(dst, dtype=x.dtype), dst, num_segments=n)
            dinv = jnp.where(deg > 0, jax.lax.rsqrt(deg), 0.0)
            norm = dinv[src] * dinv[dst]
            h = x @ W
            msg = h[src] * norm[:, None]
            agg = jax.ops.segment_sum(msg, dst, num_segments=n)
            return agg + b
        key = jax.random.key(seed)
        k1, k2, k3, k4 = jax.random.split(key, 4)
        x = jax.random.normal(k1, (N_NODES, IN_DIM), dtype=jnp.float32)
        edge_index = jax.random.randint(k2, (2, N_EDGES), 0, N_NODES, dtype=jnp.int32)
        W_conv = jax.random.normal(k3, (IN_DIM, HID_DIM), dtype=jnp.float32) * (1.0 / np.sqrt(IN_DIM))
        b_conv = jnp.zeros((HID_DIM,), dtype=jnp.float32)
        W_lin = jax.random.normal(k4, (HID_DIM, OUT_DIM), dtype=jnp.float32) * (1.0 / np.sqrt(HID_DIM))
        b_lin = jnp.zeros((OUT_DIM,), dtype=jnp.float32)
        return {'x': x, 'edge_index': edge_index, 'W_conv': W_conv, 'b_conv': b_conv, 'W_lin': W_lin, 'b_lin': b_lin}
    _L1_gnn_all = _L1_gnn_setup()
    _L1_gnn_in = {k: v for k, v in _L1_gnn_all.items() if k in ('W_conv', 'b_conv', 'W_lin', 'b_lin')}
    del _L1_gnn_all
    return {'x': x, 'src': src, 'dst': dst, 'edge_attr_32': edge_attr_32, 'L0_gnn_W_emb': _L0_gnn_in['W_emb'], 'L0_gnn_b_emb': _L0_gnn_in['b_emb'], 'L0_gnn_W_temb': _L0_gnn_in['W_temb'], 'L0_gnn_b_temb': _L0_gnn_in['b_temb'], 'L0_gnn_W_tattr': _L0_gnn_in['W_tattr'], 'L0_gnn_b_tattr': _L0_gnn_in['b_tattr'], 'L0_gnn_W_gate': _L0_gnn_in['W_gate'], 'L0_gnn_b_gate': _L0_gnn_in['b_gate'], 'L0_gnn_W_l': _L0_gnn_in['W_l'], 'L0_gnn_b_l': _L0_gnn_in['b_l'], 'L0_gnn_W_r': _L0_gnn_in['W_r'], 'L0_gnn_gamma': _L0_gnn_in['gamma'], 'L0_gnn_beta': _L0_gnn_in['beta'], 'L1_gnn_W_conv': _L1_gnn_in['W_conv'], 'L1_gnn_b_conv': _L1_gnn_in['b_conv'], 'L1_gnn_W_lin': _L1_gnn_in['W_lin'], 'L1_gnn_b_lin': _L1_gnn_in['b_lin']}

def reference(x, src, dst, edge_attr_32, L0_gnn_W_emb, L0_gnn_b_emb, L0_gnn_W_temb, L0_gnn_b_temb, L0_gnn_W_tattr, L0_gnn_b_tattr, L0_gnn_W_gate, L0_gnn_b_gate, L0_gnn_W_l, L0_gnn_b_l, L0_gnn_W_r, L0_gnn_gamma, L0_gnn_beta, L1_gnn_W_conv, L1_gnn_b_conv, L1_gnn_W_lin, L1_gnn_b_lin):
    import jax
    import jax.numpy as jnp

    def _L0_gnn_ref(x, edge_attr, W_emb, b_emb, W_temb, b_temb, W_tattr, b_tattr, W_gate, b_gate, W_l, b_l, W_r, gamma, beta, edge_index):
        import jax, jax.numpy as jnp
        import numpy as np
        BN_EPS = 1e-05
        N = x.shape[0]
        row, col = (edge_index[0], edge_index[1])
        emb = jax.nn.relu(edge_attr @ W_emb + b_emb)
        t_attr = edge_attr @ W_tattr + b_tattr
        t = emb @ W_temb + b_temb + t_attr
        agg = jax.ops.segment_sum(x[row], col, num_segments=N)
        cnt = jax.ops.segment_sum(jnp.ones_like(col, x.dtype), col, num_segments=N)
        agg = agg / jnp.maximum(cnt, 1.0)[:, None]
        out = agg @ W_l + b_l + x @ W_r
        comb = jnp.concatenate([out[col], t, t_attr], axis=-1)
        gate = jax.nn.sigmoid(comb @ W_gate + b_gate)
        out = out + jax.ops.segment_sum(gate * t, col, num_segments=N)
        mu = jnp.mean(out, axis=0)
        var = jnp.mean((out - mu) ** 2, axis=0)
        out = (out - mu) * jax.lax.rsqrt(var + BN_EPS) * gamma + beta
        return jax.nn.relu(2.0 * out)

    def _L1_gnn_ref(x, edge_index, W_conv, b_conv, W_lin, b_lin):
        import jax, jax.numpy as jnp
        import numpy as np
        N_NODES = 12500
        N_EDGES = 200000
        IN_DIM, HID_DIM, OUT_DIM = (128, 64, 128)

        def gcn_conv(x, edge_index, W, b):
            n = x.shape[0]
            loop = jnp.arange(n, dtype=edge_index.dtype)
            src = jnp.concatenate([edge_index[0], loop])
            dst = jnp.concatenate([edge_index[1], loop])
            deg = jax.ops.segment_sum(jnp.ones_like(dst, dtype=x.dtype), dst, num_segments=n)
            dinv = jnp.where(deg > 0, jax.lax.rsqrt(deg), 0.0)
            norm = dinv[src] * dinv[dst]
            h = x @ W
            msg = h[src] * norm[:, None]
            agg = jax.ops.segment_sum(msg, dst, num_segments=n)
            return agg + b
        h = gcn_conv(x, edge_index, W_conv, b_conv)
        h = jax.nn.relu(h)
        return h @ W_lin + b_lin
    edge_index = jnp.stack([src, dst])
    h = jnp.maximum(_layernorm(x, axis=-1), 0.0)
    x = x + _L0_gnn_ref(h, edge_attr_32, L0_gnn_W_emb, L0_gnn_b_emb, L0_gnn_W_temb, L0_gnn_b_temb, L0_gnn_W_tattr, L0_gnn_b_tattr, L0_gnn_W_gate, L0_gnn_b_gate, L0_gnn_W_l, L0_gnn_b_l, L0_gnn_W_r, L0_gnn_gamma, L0_gnn_beta, edge_index)
    h = jnp.maximum(_layernorm(x, axis=-1), 0.0)
    x = x + _L1_gnn_ref(h, edge_index, L1_gnn_W_conv, L1_gnn_b_conv, L1_gnn_W_lin, L1_gnn_b_lin)
    return x

_drawn_inputs = setup_inputs


def setup_inputs(seed=0):
    import zlib

    import numpy as np

    out = dict(_drawn_inputs(seed))
    spreads = {'L0_gnn_b_emb': (0.0, 0.1),
     'L0_gnn_b_temb': (0.0, 0.1),
     'L0_gnn_b_tattr': (0.0, 0.1),
     'L0_gnn_b_gate': (0.0, 0.686),
     'L0_gnn_b_l': (0.0, 0.8),
     'L0_gnn_gamma': (1.0, 0.2),
     'L0_gnn_beta': (0.0, 0.1),
     'L1_gnn_b_conv': (0.0, 0.1),
     'L1_gnn_b_lin': (0.0, 0.1)}
    factors = {}
    for name, (base, spread) in spreads.items():
        noise = np.random.default_rng([zlib.crc32(name.encode()), seed]).standard_normal(out[name].shape)
        drawn = base * np.exp(spread * noise) if base else spread * noise
        out[name] = jnp.asarray(drawn.astype(out[name].dtype))
    for name, factor in factors.items():
        out[name] = (out[name] * factor).astype(out[name].dtype)
    return out
```

```python
from contextlib import ExitStack

import numpy as np

import concourse.bass as bass
from concourse import mybir

F32 = mybir.dt.float32
I32 = mybir.dt.int32
BF16 = mybir.dt.bfloat16
ALU = mybir.AluOpType
ACT = mybir.ActivationFunctionType

P = 128
N = 12500
E = 400000
D = 128
HID = 64
EA, EE = 32, 16
ONE = EA + EE
EPS = 1e-5

W = 64
CT = 4
EC = CT * P
CHUNKS = -(-E // EC) + (-(-E // EC)) % 4
U = 4
LAG = 12
STEPS = CHUNKS + 16
FRONT = 16
SLOTS = FRONT + STEPS + 4

NT = -(-N // P)
NP = NT * P
NW = NP + W
GT = 7
GC = GT * P
GROUPS = NT // GT
HALF = GC // 2
BN_PIECE = 500

KEEP = ["W_l", "W_g1", "emb", "ident", "ones", "lin", "conv", "iota", "b_l", "gamma", "beta",
        "b_conv", "pmod", "eps", "b_emb"]
KEEP_W = [D, D, D, P, P, D, HID, W, 1, 1, 1, 1, 1, 1, 1]
ONCE = ["AT", "BT", "CT", "W_g2", "W_g3", "W_r", "e_one", "b_gate"]
ONCE_W = [P, P, P, D, D, D, P, D]


def columns(names, widths):
    at, out = 0, {}
    for n, w in zip(names, widths):
        out[n] = (at, at + w)
        at += w
    return out, at


KEEP_AT, KEEP_N = columns(KEEP, KEEP_W)
ONCE_AT, ONCE_N = columns(ONCE, ONCE_W)
assert GROUPS * GT == NT and CHUNKS % U == 0 and STEPS % U == 0 and N % BN_PIECE == 0


def wait_alone(eng, sem, value, passed):
    eng.wait_ge(sem, value)
    eng.sem_inc(passed, 1)


class Chain:

    def __init__(self, eng, sem, turn, per_turn, passed):
        self.eng, self.sem, self.turn, self.per_turn, self.n = eng, sem, turn, per_turn, 0
        self.passed = passed

    def then(self, ins):
        self.n += 1
        ins.then_inc(self.sem, 1)

    def wait(self):
        wait_alone(self.eng, self.sem, self.turn * self.per_turn + self.n, self.passed)

    def close(self):
        assert self.n == self.per_turn, self.n


def gnn_two_layers(nc, x, src, dst, dst_row, base, ea, ea4, keep, once, out):
    r_dram = nc.dram_tensor("r_dram", (P, NW), F32).ap()
    h_dram = nc.dram_tensor("h_dram", (NP, 3 * D), BF16).ap()
    hs_dram = nc.dram_tensor("hs_dram", (NP, HID), F32).ap()
    xg = x.rearrange("(g j p) d -> g p j d", j=GT, p=P)
    hg = h_dram.rearrange("(g j p) d -> g p j d", j=GT, p=P)
    hsg = hs_dram.rearrange("(g j p) d -> g p j d", j=GT, p=P)
    og = out.rearrange("(g j p) d -> g p j d", j=GT, p=P)

    with ExitStack() as kept:
        def sb(name, shape, dt=F32, ctx=kept):
            return ctx.enter_context(nc.sbuf_tensor(name, shape, dt))

        def ps(name, shape, ctx):
            return ctx.enter_context(nc.psum_tensor(name, shape, F32))

        def sem(name):
            return kept.enter_context(nc.semaphore(name))

        passed = sem("passed")

        ac = sb("ac", [P, 2, NW])
        gs = sb("gs", [P, NW])
        rel = sb("rel", [P, SLOTS, CT], I32)
        relf = rel[:, :, :].bitcast(F32)
        base_p = sb("base_p", [P, SLOTS])
        base_i = sb("base_i", [1, SLOTS], I32)
        kp = sb("kp", [P, KEEP_N])
        wt = sb("wt", [P, 2 * D])

        def k(name, rows=P):
            a, b = KEEP_AT[name]
            return kp[0:rows, a:b]

        bn = sb("bn", [P, 8])

        with ExitStack() as c0:
            xb = sb("x0", [P, 2, GT, D], ctx=c0)
            hb = sb("h0", [P, GT, D], ctx=c0)
            hr = sb("hr0", [P, GT, D], ctx=c0)
            hp = sb("hp0", [P, GT, 3 * D], BF16, ctx=c0)
            hT = sb("hT0", [P, GC], ctx=c0)
            rT = sb("rT0", [P, GC], ctx=c0)
            st = sb("st0", [P, GT, 6], ctx=c0)
            mv = sb("mv0", [P, GT, 2], ctx=c0)
            rs = sb("rs0", [P, GT], ctx=c0)
            nb = sb("nb0", [P, GT], ctx=c0)
            sd = sb("sd0", [P, GT], ctx=c0)
            zero = sb("zero0", [P, W], ctx=c0)
            on = gs[:, 0:ONCE_N]
            baseb = gs[:, ONCE_N:ONCE_N + SLOTS].bitcast(I32)
            pT = ps("pT0", [P, 1024], c0)
            pR = ps("pR0", [P, 1024], c0)
            pW = ps("pW0", [P, 512], c0)

            def o(name, rows=P):
                a, b = ONCE_AT[name]
                return on[0:rows, a:b]

            consts_in = sem("consts_in")
            tables_in = sem("tables_in")
            x_in = [sem("x_in0"), sem("x_in1")]
            h_out = sem("h_out")
            hi_ready = sem("hi_ready")
            rest_ready = sem("rest_ready")
            mid_ready = sem("mid_ready")
            lo_ready = sem("lo_ready")
            ones_ready = sem("ones_ready")
            h_free = sem("h_free")
            rT_free = sem("rT_free")
            r_out = sem("r_out")
            pad_out = sem("pad_out")
            chain0 = sem("chain0")
            stats_ready = sem("stats_ready")
            std_ready = sem("std_ready")
            ready_stats = sem("ready_stats")
            ready_h = sem("ready_h")
            ready_hT = sem("ready_hT")
            hT_copied = sem("hT_copied")
            ready_r = sem("ready_r")
            ready_rT = sem("ready_rT")
            ready_wt = sem("ready_wt")
            zeroed = sem("zeroed")
            setup = sem("setup")
            T0 = GROUPS // 2
            with nc.Block() as block:
                @block.sync
                def _(e):
                    e.dma_start(kp[:, :], keep).then_inc(consts_in, 16)
                    e.dma_start(on, once).then_inc(consts_in, 16)
                    e.dma_start(rel[:, :, :], dst).then_inc(tables_in, 16)
                    e.dma_start(base_i[:, :], base).then_inc(tables_in, 16)
                    e.dma_start(baseb, base.to_broadcast((P, SLOTS))).then_inc(tables_in, 16)
                    with e.Fori(0, T0) as t:
                        for u in range(2):
                            e.wait_ge(ready_h, t * 2 + (u + 1))
                            e.dma_start(xb[:, u, :, :], xg[t * 2 + u]).then_inc(x_in[u], 16)

                @block.gpsimd
                def _(e):
                    e.sem_inc(h_free, 1)
                    e.sem_inc(rT_free, 1)
                    e.memset(zero[:, :], 0.0).then_inc(zeroed, 1)
                    e.memset(ac[:, :, :], 0.0).then_inc(zeroed, 1)
                    e.wait_ge(zeroed, 2)
                    e.dma_start(r_dram[:, NP:NW], zero[:, :]).then_inc(pad_out, 16)
                    e.wait_ge(pad_out, 16)
                    with e.Fori(0, T0) as t:
                        for u in range(2):
                            e.wait_ge(hi_ready, t * 2 + (u + 1))
                            e.tensor_tensor(hr[:, :, :], hb[:, :, :], hp[:, :, 0:D], ALU.subtract)\
                                .then_inc(rest_ready, 1)
                            e.wait_ge(lo_ready, t * 2 + (u + 1))
                            e.dma_start(hg[t * 2 + u], hp[:, :, :]).then_inc(h_out, 16)
                            e.wait_ge(ready_rT, t * 2 + (u + 1))
                            e.dma_start(r_dram[:, bass.ds((t * 2 + u) * GC, GC)], rT[:, :]).then_inc(r_out, 16)
                            e.wait_ge(h_out, t * 32 + (16 * u + 16))
                            e.sem_inc(h_free, 1)
                            e.wait_ge(r_out, t * 32 + (16 * u + 16))
                            e.sem_inc(rT_free, 1)

                @block.vector
                def _(e):
                    e.sem_inc(ready_h, 2)
                    e.wait_ge(tables_in, 48)
                    e.tensor_tensor(relf, rel[:, :, :],
                                    baseb.rearrange("p (s o) -> p s o", o=1).to_broadcast((P, SLOTS, CT)),
                                    ALU.subtract).then_inc(setup, 1)
                    e.wait_ge(consts_in, 32)
                    e.tensor_scalar(base_p[:, :], baseb, k("pmod"), None, ALU.add).then_inc(setup, 1)
                    e.wait_ge(ready_wt, 1)
                    e.tensor_copy(wt[:, :], pW[:, 0:2 * D]).then_inc(setup, 1)
                    with e.Fori(0, T0) as t:
                        ch = Chain(e, chain0, t, 6, passed)
                        for u in range(2):
                            wait_alone(e, x_in[u], t * 16 + 16, passed)
                            for j in range(GT):
                                ins = e.bn_stats(st[:, j, :], xb[:, u, j, :])
                            ch.then(ins)
                            ch.wait()
                            wait_alone(e, ready_h, t * 2 + (u + 2), passed)
                            for j in range(GT):
                                ins = e.bn_aggr(mv[:, j, :], st[:, j, :])
                            ch.then(ins)
                            ch.wait()
                            e.sem_inc(stats_ready, 1)
                            e.wait_ge(std_ready, t * 2 + (u + 1))
                            ch.then(e.reciprocal(rs[:, :], sd[:, :]))
                            ch.wait()
                            e.scalar_tensor_tensor(out=nb[:, :], in0=mv[:, :, 0], scalar=-1.0,
                                                   in1=rs[:, :], op0=ALU.mult, op1=ALU.mult)\
                                .then_inc(ready_stats, 1)
                            e.wait_ge(mid_ready, t * 2 + (u + 1))
                            e.tensor_tensor(hp[:, :, 2 * D:3 * D], hr[:, :, :], hp[:, :, D:2 * D],
                                            ALU.subtract).then_inc(lo_ready, 1)
                            e.wait_ge(ready_hT, t * 2 + (u + 1))
                            e.tensor_copy(hT[:, :], pT[:, 0:GC]).then_inc(hT_copied, 1)
                            e.wait_ge(ready_r, t * 2 + (u + 1))
                            e.wait_ge(rT_free, t * 2 + (u + 1))
                            e.tensor_scalar(rT[:, :].rearrange("p (a b) -> p a b", a=2),
                                            pR[:, :].rearrange("p (a b) -> p a b", a=2)[:, :, 0:HALF],
                                            k("b_l"), None, ALU.add).then_inc(ready_rT, 1)
                        ch.close()
                    e.wait_ge(ready_r, GROUPS)
                    e.memset(gs[:, :], 0.0).then_inc(setup, 1)
                    e.wait_ge(setup, 4)

                @block.scalar
                def _(e):
                    with e.Fori(0, T0) as t:
                        for u in range(2):
                            e.wait_ge(stats_ready, t * 2 + (u + 1))
                            e.activation(sd[:, :], mv[:, :, 1], ACT.Sqrt, bias=k("eps"))\
                                .then_inc(std_ready, 1)
                            e.wait_ge(ready_stats, t * 2 + (u + 1))
                            e.wait_ge(h_free, t * 2 + (u + 1))
                            e.wait_ge(hT_copied, t * 2 + (u + 1))
                            for j in range(GT):
                                ins = e.activation(hb[:, j, :], xb[:, u, j, :], ACT.Relu,
                                                   bias=nb[:, j:j + 1], scale=rs[:, j:j + 1])
                            ins.then_inc(ready_h, 1)
                            e.wait_ge(ready_h, t * 2 + (u + 3))
                            e.activation(hp[:, :, 0:D], hb[:, :, :], ACT.Copy).then_inc(hi_ready, 1)
                            e.wait_ge(rest_ready, t * 2 + (u + 1))
                            e.activation(hp[:, :, D:2 * D], hr[:, :, :], ACT.Copy).then_inc(mid_ready, 1)

                @block.tensor
                def _(e):
                    e.sem_inc(hT_copied, 1)
                    e.wait_ge(consts_in, 32)
                    e.matmul(pW[:, D:2 * D], o("AT"), k("ident"), start=True, stop=False)
                    e.matmul(pW[:, D:2 * D], o("CT"), k("ident"), start=False, stop=True)
                    e.matmul(pW[:, 0:D], o("AT"), o("W_g2"), start=True, stop=False)
                    e.matmul(pW[:, 0:D], o("CT"), o("W_g2"), start=False, stop=False)
                    e.matmul(pW[:, 0:D], o("BT"), o("W_g3"), start=False, stop=False)
                    e.matmul(pW[:, 0:D], o("e_one"), o("b_gate"), start=False, stop=True).then_inc(ready_wt, 1)
                    with e.Fori(0, T0) as t:
                        for u in range(2):
                            e.wait_ge(ready_h, t * 2 + (u + 3))
                            for j in range(GT):
                                ins = e.transpose(pT[:, j * P:(j + 1) * P], hb[:, j, :], k("ident"))
                            ins.then_inc(ready_hT, 1)
                            e.wait_ge(hT_copied, t * 2 + (u + 2))
                            for b in range(2):
                                ins = e.matmul(pR[:, b * 512:b * 512 + HALF], o("W_r"),
                                               hT[:, b * HALF:(b + 1) * HALF], start=True, stop=True)
                            ins.then_inc(ready_r, 1)

        with ExitStack() as c1:
            g = sb("g", [P, U, CT, 3 * D], BF16, ctx=c1)
            ix = sb("ix", [P, 2, 2 * CT], I32, ctx=c1)
            oh1 = sb("oh1", [P, 2, CT, W], BF16, ctx=c1)
            oh2 = sb("oh2", [P, 2, CT, W], ctx=c1)
            fs = sb("fs", [P, U, EC], ctx=c1)
            e4 = sb("e4", [P, EC], ctx=c1)
            onesb = sb("onesb", [P, P], BF16, ctx=c1)
            rw = sb("rw", [P, 2, 2, W], ctx=c1)
            mean = sb("mean", [P, W], ctx=c1)
            rc = sb("rc", [P, 2, W], ctx=c1)
            ow = sb("ow", [P, 2, W], ctx=c1)
            gm = sb("gm", [P, 2, CT, D], ctx=c1)
            pF = ps("pF", [P, 2, CT, 2, D], c1)
            pA = ps("pA", [P, 512], c1)
            pE = ps("pE", [P, 512], c1)
            pG = ps("pG", [P, 512], c1)
            pM = ps("pM", [P, 512], c1)

            ix_in = [sem("ix_in0"), sem("ix_in1")]
            g_in = [sem(f"g_in{u}") for u in range(U)]
            ea_in = [sem("ea_in0"), sem("ea_in1")]
            db_in = [sem("db_in0"), sem("db_in1")]
            e4_in = sem("e4_in")
            rw_in = [sem("rw_in0"), sem("rw_in1")]
            oh1_ready = sem("oh1_ready")
            sums_ready = sem("sums_ready")
            sums_added = sem("sums_added")
            emb_in = sem("emb_in")
            emb_ready = sem("emb_ready")
            mean_ready = sem("mean_ready")
            lin_ready = sem("lin_ready")
            ow_ready = sem("ow_ready")
            gw_in = sem("gw_in")
            gw_ready = sem("gw_ready")
            ohT_ready = sem("ohT_ready")
            oh2_ready = sem("oh2_ready")
            feat_ready = sem("feat_ready")
            gate_ready = sem("gate_ready")
            msg_ready = sem("msg_ready")
            gsum_ready = sem("gsum_ready")
            gsum_added = sem("gsum_added")
            chain1 = sem("chain1")
            cleared = sem("cleared")
            CLEARS = 4
            TURNS = STEPS // U

            def slot(t, u, shift):
                return t * U + (u + FRONT + shift)

            def load_base(e, s):
                return e.value_load(base_i[0:1, bass.ds(s, 1)], min_val=0, max_val=NW - W)

            with nc.Block() as block:
                @block.sync
                def _(e):
                    e.wait_ge(cleared, CLEARS)
                    e.dma_start(e4[:, :], ea4[:, 0, :]).then_inc(e4_in, 16)
                    with e.Fori(0, TURNS) as t:
                        for h in range(2):
                            s0 = slot(t, 2 * h, 1 - LAG)
                            e.wait_ge(sums_ready, t * U + (2 * h + 2))
                            e.dma_start(ix[:, h, :], src[:, bass.ds(t * (U * CT) + 2 * h * CT, 2 * CT)])\
                                .then_inc(ix_in[h], 16)
                            e.wait_ge(feat_ready, t * U + (2 * h + 3))
                            e.dma_start(fs[0:EA, 2 * h:2 * h + 2, :], ea[:, bass.ds(s0, 2), :])\
                                .then_inc(ea_in[h], 16)
                            e.dma_start(fs[64:64 + W, 2 * h:2 * h + 2, :].bitcast(I32),
                                        dst_row[0:1, bass.ds(s0, 2), :].to_broadcast((W, 2, EC)))\
                                .then_inc(db_in[h], 16)
                            if h == 1:
                                e.wait_ge(emb_in, t + 1)
                                e.dma_start(e4[:, :], ea4[:, bass.ds(t + 1, 1), :]
                                            .rearrange("p o c -> p (o c)")).then_inc(e4_in, 16)
                            e.wait_ge(ow_ready, t * U + (2 * h + 2))
                            for v in range(2):
                                first = load_base(e, slot(t, 2 * h + v, 1 - LAG))
                                e.dma_start(rw[:, h, v, :], r_dram[:, bass.ds(first, W)]).then_inc(rw_in[h], 16)

                @block.gpsimd
                def _(e):
                    with e.Fori(0, TURNS) as t:
                        for u in range(U):
                            if u % 2 == 0:
                                wait_alone(e, ix_in[u // 2], t * 16 + 16, passed)
                            wait_alone(e, sums_ready, t * U + (u + 1), passed)
                            for j in range(CT):
                                c = (u % 2) * CT + j
                                e.indirect_dma_start(
                                    g[:, u, j, :], None, h_dram,
                                    bass.IndirectOffsetOnAxis(ap=ix[:, u // 2, c:c + 1], axis=0)
                                ).then_inc(g_in[u], 16)

                @block.tensor
                def _(e):
                    e.sem_inc(sums_ready, U)
                    e.sem_inc(feat_ready, U)
                    e.sem_inc(gsum_ready, 1)
                    e.wait_ge(cleared, CLEARS)
                    with e.Fori(0, TURNS) as t:
                        for u in range(U):
                            b, h, v = u % 2, u // 2, u % 2
                            e.wait_ge(oh1_ready, t * U + (u + 1))
                            e.wait_ge(sums_added, t * U + (u + 1))
                            e.wait_ge(g_in[u], t * (16 * CT) + 16 * CT)
                            for j in range(CT):
                                for part in range(3):
                                    e.matmul(pA[:, 0:W], g[:, u, j, part * D:(part + 1) * D], oh1[:, b, j, :],
                                             start=(j == 0 and part == 0), stop=(j == CT - 1 and part == 2))
                            for j in range(CT):
                                ins = e.matmul(pA[:, W:2 * W], onesb[:, :], oh1[:, b, j, :],
                                               start=(j == 0), stop=(j == CT - 1))
                            ins.then_inc(sums_ready, 1)
                            e.wait_ge(emb_ready, t * U + (u + 1))
                            e.wait_ge(gw_ready, t * U + (u + 1))
                            e.wait_ge(ohT_ready, t * U + (u + 1))
                            for j in range(CT):
                                ins = e.matmul(pF[:, b, j, :, :].rearrange("p a d -> p (a d)"),
                                               fs[:, (u - 1) % U, j * P:(j + 1) * P], wt[:, :],
                                               start=True, stop=True)
                            ins.then_inc(feat_ready, 1)
                            if u == 0:
                                wait_alone(e, e4_in, t * 16 + 16, passed)
                                e.matmul(pE[:, :], k("emb"), e4[:, :], start=True, stop=True)\
                                    .then_inc(emb_in, 1)
                            e.wait_ge(mean_ready, t * U + (u + 1))
                            e.wait_ge(ow_ready, t * U + (u + U))
                            e.matmul(pG[:, D:D + W], k("W_l"), mean[:, :], start=True, stop=True)\
                                .then_inc(lin_ready, 1)
                            e.wait_ge(msg_ready, t * U + (u + 1))
                            e.wait_ge(oh2_ready, t * U + (u + 1))
                            e.wait_ge(gsum_added, t * U + (u + 1))
                            for j in range(CT):
                                ins = e.matmul(pM[:, 0:W],
                                               gm[:, 1 - b, j, :], oh2[:, 1 - b, j, :],
                                               start=(j == 0), stop=(j == CT - 1))
                            ins.then_inc(gsum_ready, 1)
                            e.wait_ge(ow_ready, t * U + (u + U + 1))
                            e.matmul(pG[:, 0:D], ow[:, :, :].rearrange("p a w -> p (a w)"), k("W_g1"),
                                     start=True, stop=True).then_inc(gw_in, 1)

                @block.scalar
                def _(e):
                    e.wait_ge(cleared, CLEARS)
                    e.sem_inc(emb_ready, 1)
                    e.sem_inc(gw_ready, 1)
                    with e.Fori(0, TURNS) as t:
                        for u in range(U):
                            b, h, v = u % 2, u // 2, u % 2
                            e.wait_ge(feat_ready, t * U + (u + U + 1))
                            e.wait_ge(gsum_ready, t * U + (u + 1))
                            e.activation(gm[:, b, :, :], pF[:, b, :, 0, :], ACT.Sigmoid).then_inc(gate_ready, 1)
                            e.wait_ge(emb_in, t + 1)
                            e.wait_ge(ea_in[h], t * 16 + 16)
                            e.activation(fs[EA:ONE, u, :], pE[EA * u:EA * u + EE, :], ACT.Relu,
                                         bias=k("b_emb")[EA * u:EA * u + EE, :]).then_inc(emb_ready, 1)
                            e.wait_ge(gw_in, t * U + (u + 1))
                            e.activation(wt[64:P, 0:D], pG[64:P, 0:D], ACT.Copy).then_inc(gw_ready, 1)

                @block.vector
                def _(e):
                    e.memset(fs[:, :, :], 1.0).then_inc(cleared, 1)
                    e.memset(onesb[:, :], 1.0).then_inc(cleared, 1)
                    e.memset(gm[:, :, :, :], 0.0).then_inc(cleared, 1)
                    e.memset(oh2[:, :, :, :], 0.0).then_inc(cleared, 1)
                    e.wait_ge(cleared, CLEARS)
                    e.sem_inc(sums_added, 1)
                    e.sem_inc(gsum_added, 1)
                    e.sem_inc(ohT_ready, 1)
                    e.sem_inc(ow_ready, U)
                    e.sem_inc(msg_ready, 1)
                    e.sem_inc(oh2_ready, 1)

                    def one_hot(to, s):
                        return e.tensor_tensor(
                            to, relf[:, bass.ds(s, 1), :].rearrange("p s (c o) -> p (s c) o", o=1)
                            .to_broadcast((P, CT, W)),
                            k("iota").rearrange("p (o w) -> p o w", o=1).to_broadcast((P, CT, W)),
                            ALU.is_equal)

                    one_hot(oh1[:, 0, :, :], FRONT).then_inc(oh1_ready, 1)
                    with e.Fori(0, TURNS) as t:
                        ch = Chain(e, chain1, t, 2 * U, passed)
                        for u in range(U):
                            b, h, v = u % 2, u // 2, u % 2
                            e.wait_ge(db_in[h], t * 16 + 16)
                            e.tensor_scalar(fs[64:64 + W, u, :], fs[64:64 + W, u, :].bitcast(I32),
                                            base_p[64:64 + W, bass.ds(slot(t, u, 1 - LAG), 1)], None,
                                            ALU.is_equal).then_inc(ohT_ready, 1)
                            e.wait_ge(sums_added, t * U + (u + 1))
                            wa = load_base(e, slot(t, u, 1 - LAG))
                            ch.then(e.tensor_scalar(rc[:, 0, :], ac[:, 1, bass.ds(wa, W)], 1.0, None, ALU.max))
                            ch.wait()
                            ch.then(e.reciprocal(rc[:, 1, :], rc[:, 0, :]))
                            ch.wait()
                            e.tensor_tensor(mean[:, :], ac[:, 0, bass.ds(wa, W)], rc[:, 1, :],
                                            ALU.mult).then_inc(mean_ready, 1)
                            e.wait_ge(gsum_ready, t * U + (u + 1))
                            one_hot(oh2[:, b, :, :], slot(t, u, -LAG)).then_inc(oh2_ready, 1)
                            wk = load_base(e, slot(t, u, 0))
                            e.wait_ge(sums_ready, t * U + (u + U + 1))
                            e.wait_ge(mean_ready, t * U + (u + 1))
                            to = ac[:, :, bass.ds(wk, W)]
                            e.tensor_tensor(to, to, pA[:, 0:2 * W].rearrange("p (a w) -> p a w", a=2),
                                            ALU.add).then_inc(sums_added, 1)
                            one_hot(oh1[:, 1 - b, :, :], slot(t, u, 1)).then_inc(oh1_ready, 1)
                            e.wait_ge(rw_in[h], t * 32 + 32)
                            e.wait_ge(lin_ready, t * U + (u + 1))
                            e.tensor_tensor(ow[:, :, :],
                                            pG[:, D:D + W].rearrange("p (o w) -> p o w", o=1).to_broadcast((P, 2, W)),
                                            rw[:, h, v:v + 1, :].to_broadcast((P, 2, W)),
                                            ALU.add).then_inc(ow_ready, 1)
                            e.wait_ge(gate_ready, t * U + (u + 1))
                            e.tensor_tensor(gm[:, b, :, :], gm[:, b, :, :], pF[:, b, :, 1, :],
                                            ALU.mult).then_inc(msg_ready, 1)
                            wg = load_base(e, slot(t, u, -1 - LAG))
                            e.wait_ge(gsum_ready, t * U + (u + 2))
                            e.wait_ge(gsum_added, t * U + (u + 1))
                            to = gs[:, bass.ds(wg, W)]
                            e.tensor_tensor(to, to, pM[:, 0:W], ALU.add).then_inc(gsum_added, 1)
                        ch.close()

        with ExitStack() as c2:
            rb = sb("rb", [P, GC], ctx=c2)
            mb = sb("mb", [P, 2, GC], ctx=c2)
            bs = sb("bs", [P, N // BN_PIECE, 6], ctx=c2)
            pL = ps("pL", [P, 2, 512], c2)
            r_in = sem("r_in")
            means_ready = sem("means_ready")
            deg_ready = sem("deg_ready")
            bn_std = sem("bn_std")
            dg = sb("dg", [P, GC], ctx=c2)
            lin2_ready = sem("lin2_ready")
            group_done = sem("group_done")
            chain2 = sem("chain2")
            bn_chain = sem("bn_chain")
            with nc.Block() as block:
                @block.sync
                def _(e):
                    with e.Fori(0, GROUPS) as t:
                        e.wait_ge(group_done, t + 1)
                        e.dma_start(rb[:, :], r_dram[:, bass.ds(t * GC, GC)]).then_inc(r_in, 16)

                @block.tensor
                def _(e):
                    with e.Fori(0, GROUPS) as t:
                        e.wait_ge(means_ready, t + 1)
                        for b in range(2):
                            ins = e.matmul(pL[:, b, 0:HALF], k("W_l"), mb[:, 1, b * HALF:(b + 1) * HALF],
                                           start=True, stop=True)
                        ins.then_inc(lin2_ready, 1)

                @block.scalar
                def _(e):
                    with e.Fori(0, GROUPS) as t:
                        e.wait_ge(group_done, t + 1)
                        e.activation(dg[:, :], ac[:, 1, bass.ds(t * GC, GC)], ACT.Sqrt,
                                     bias=k("ones")[:, 0:1]).then_inc(deg_ready, 1)
                    e.wait_ge(bn_chain, 2)
                    e.activation(bn[:, 7:8], bn[:, 1:2], ACT.Sqrt, bias=k("eps")).then_inc(bn_std, 1)

                @block.vector
                def _(e):
                    e.sem_inc(group_done, 1)
                    with e.Fori(0, GROUPS) as t:
                        ch = Chain(e, chain2, t, 5, passed)
                        cols = bass.ds(t * GC, GC)
                        ch.then(e.tensor_scalar(mb[:, 0, :], ac[:, 1, cols], 1.0, None, ALU.max))
                        ch.wait()
                        ch.then(e.reciprocal(mb[:, 1, :], mb[:, 0, :]))
                        ch.wait()
                        e.tensor_tensor(mb[:, 1, :], ac[:, 0, cols], mb[:, 1, :], ALU.mult).then_inc(means_ready, 1)
                        wait_alone(e, deg_ready, t + 1, passed)
                        ch.then(e.reciprocal(ac[:, 1, cols], dg[:, :]))
                        e.wait_ge(r_in, t * 16 + 16)
                        ch.then(e.tensor_tensor(gs[:, cols], gs[:, cols], rb[:, :], ALU.add))
                        ch.wait()
                        e.wait_ge(lin2_ready, t + 1)
                        to = gs[:, cols].rearrange("p (a b) -> p a b", a=2)
                        ch.then(e.tensor_tensor(to, to, pL[:, :, 0:HALF], ALU.add))
                        ch.wait()
                        e.sem_inc(group_done, 1)
                        ch.close()
                    for i in range(N // BN_PIECE):
                        ins = e.bn_stats(bs[:, i, :], gs[:, i * BN_PIECE:(i + 1) * BN_PIECE])
                    ins.then_inc(bn_chain, 1)
                    e.wait_ge(bn_chain, 1)
                    e.bn_aggr(bn[:, 0:2], bs[:, :, :]).then_inc(bn_chain, 1)
                    e.wait_ge(bn_std, 1)
                    e.reciprocal(bn[:, 2:3], bn[:, 7:8]).then_inc(bn_chain, 1)
                    e.wait_ge(bn_chain, 3)
                    e.scalar_tensor_tensor(out=bn[:, 3:4], in0=bn[:, 2:3], scalar=2.0, in1=k("gamma"),
                                           op0=ALU.mult, op1=ALU.mult).then_inc(bn_chain, 1)
                    e.tensor_scalar(bn[:, 4:5], k("beta"), 2.0, None, ALU.mult).then_inc(bn_chain, 1)
                    e.wait_ge(bn_chain, 5)
                    e.tensor_tensor(bn[:, 5:6], bn[:, 0:1], bn[:, 3:4], ALU.mult).then_inc(bn_chain, 1)
                    e.wait_ge(bn_chain, 6)
                    e.tensor_tensor(bn[:, 6:7], bn[:, 4:5], bn[:, 5:6], ALU.subtract).then_inc(bn_chain, 1)
                    e.wait_ge(bn_chain, 7)

        x2 = ac[:, 0, 0:NP].rearrange("p (t d) -> p t d", d=D)

        with ExitStack() as c3:
            xb = sb("x3", [P, GT, D], ctx=c3)
            yT = sb("y3", [P, GC], ctx=c3)
            hb = sb("h3", [P, GT, D], ctx=c3)
            hT = sb("hT3", [P, GC], ctx=c3)
            hsb = sb("hs3", [P, GT, HID], ctx=c3)
            st = sb("st3", [P, GT, 6], ctx=c3)
            mv = sb("mv3", [P, GT, 2], ctx=c3)
            rs = sb("rs3", [P, GT], ctx=c3)
            nb = sb("nb3", [P, GT], ctx=c3)
            dc = sb("dc3", [P, 8], ctx=c3)
            dT = sb("dT3", [P, GC], ctx=c3)
            pT = ps("pT3", [P, 1024], c3)
            pH = ps("pH3", [P, 512], c3)
            pS = ps("pS3", [HID, 2, 512], c3)
            pD = ps("pD3", [P, 8], c3)
            x3_in = sem("x3_in")
            y_ready = sem("y_ready")
            yT_ready = sem("yT_ready")
            x2_ready = sem("x2_ready")
            stats3_ready = sem("stats3_ready")
            var3_ready = sem("var3_ready")
            std3_ready = sem("std3_ready")
            sd = sb("sd3", [P, GT], ctx=c3)
            h3_ready = sem("h3_ready")
            hT3_ready = sem("hT3_ready")
            hT3_copied = sem("hT3_copied")
            conv_ready = sem("conv_ready")
            hs_ready = sem("hs_ready")
            hs_out = sem("hs_out")
            hs_free = sem("hs_free")
            chain3 = sem("chain3")
            with nc.Block() as block:
                @block.sync
                def _(e):
                    with e.Fori(0, GROUPS) as t:
                        e.wait_ge(hs_ready, t + 1)
                        e.dma_start(xb[:, :, :], xg[t]).then_inc(x3_in, 16)

                @block.gpsimd
                def _(e):
                    with e.Fori(0, GROUPS) as t:
                        e.wait_ge(hs_ready, t + 2)
                        e.dma_start(hsg[t], hsb[:, :, :]).then_inc(hs_out, 16)
                        e.wait_ge(hs_out, t * 16 + 16)
                        e.sem_inc(hs_free, 1)

                @block.scalar
                def _(e):
                    with e.Fori(0, GROUPS) as t:
                        e.wait_ge(hs_ready, t + 1)
                        e.activation(yT[:, :], gs[:, bass.ds(t * GC, GC)], ACT.Relu, bias=bn[:, 6:7],
                                     scale=bn[:, 3:4]).then_inc(y_ready, 1)
                        e.wait_ge(var3_ready, t + 1)
                        e.activation(sd[:, :], mv[:, :, 1], ACT.Sqrt, bias=k("eps")).then_inc(std3_ready, 1)
                        e.wait_ge(stats3_ready, t + 1)
                        for j in range(GT):
                            ins = e.activation(hb[:, j, :], x2[:, bass.ds(t * GT + j, 1), :]
                                               .rearrange("p o d -> p (o d)"), ACT.Relu,
                                               bias=nb[:, j:j + 1], scale=rs[:, j:j + 1])
                        ins.then_inc(h3_ready, 1)
                        e.wait_ge(hT3_ready, t + 1)
                        e.activation(hT[:, :], pT[:, 0:GC], ACT.Copy).then_inc(hT3_copied, 1)

                @block.tensor
                def _(e):
                    with e.Fori(0, GROUPS) as t:
                        e.wait_ge(y_ready, t + 1)
                        for j in range(GT):
                            ins = e.transpose(pT[:, j * P:(j + 1) * P], yT[:, j * P:(j + 1) * P], k("ident"))
                        ins.then_inc(yT_ready, 1)
                        e.wait_ge(h3_ready, t + 1)
                        for j in range(GT):
                            ins = e.transpose(pT[:, j * P:(j + 1) * P], hb[:, j, :], k("ident"))
                        ins.then_inc(hT3_ready, 1)
                        e.wait_ge(hT3_copied, t + 1)
                        for j in range(GT):
                            e.matmul(pD[:, j:j + 1], dT[:, j * P:(j + 1) * P], k("ident")[:, 0:1],
                                     start=True, stop=True)
                        for j in range(GT):
                            e.matmul(pH[:, j * HID:(j + 1) * HID], hT[:, j * P:(j + 1) * P], k("conv"),
                                     start=True, stop=True)
                        for b in range(2):
                            ins = e.matmul(pS[:, b, 0:HALF], k("conv"), hT[:, b * HALF:(b + 1) * HALF],
                                           start=True, stop=True)
                        ins.then_inc(conv_ready, 1)

                @block.vector
                def _(e):
                    e.sem_inc(hs_ready, 1)
                    e.sem_inc(hs_free, 1)
                    with e.Fori(0, GROUPS) as t:
                        ch = Chain(e, chain3, t, 6, passed)
                        cols = bass.ds(t * GC, GC)
                        x2g = x2[:, bass.ds(t * GT, GT), :]
                        e.wait_ge(x3_in, t * 16 + 16)
                        e.wait_ge(yT_ready, t + 1)
                        ch.then(e.tensor_tensor(x2g, xb[:, :, :],
                                                pT[:, 0:GC].rearrange("p (t d) -> p t d", d=D), ALU.add))
                        ch.then(e.tensor_copy(dT[:, :], ac[:, 1, cols]))
                        ch.wait()
                        for j in range(GT):
                            ins = e.bn_stats(st[:, j, :], x2[:, bass.ds(t * GT + j, 1), :]
                                             .rearrange("p o d -> p (o d)"))
                        ch.then(ins)
                        ch.wait()
                        for j in range(GT):
                            ins = e.bn_aggr(mv[:, j, :], st[:, j, :])
                        ch.then(ins)
                        ch.wait()
                        e.sem_inc(var3_ready, 1)
                        e.wait_ge(std3_ready, t + 1)
                        ch.then(e.reciprocal(rs[:, :], sd[:, :]))
                        ch.wait()
                        e.scalar_tensor_tensor(out=nb[:, :], in0=mv[:, :, 0], scalar=-1.0, in1=rs[:, :],
                                               op0=ALU.mult, op1=ALU.mult).then_inc(stats3_ready, 1)
                        e.wait_ge(conv_ready, t + 1)
                        e.tensor_tensor(gs[0:HID, cols].rearrange("p (a b) -> p a b", a=2), pS[:, :, 0:HALF],
                                        ac[0:HID, 1, cols].rearrange("p (a b) -> p a b", a=2), ALU.mult)
                        ch.then(e.tensor_copy(dc[:, 0:GT], pD[:, 0:GT]))
                        ch.wait()
                        e.wait_ge(hs_free, t + 1)
                        e.tensor_tensor(hsb[:, :, :], pH[:, 0:GT * HID].rearrange("p (t f) -> p t f", f=HID),
                                        dc[:, 0:GT].rearrange("p (t o) -> p t o", o=1)
                                        .to_broadcast((P, GT, HID)), ALU.mult).then_inc(hs_ready, 1)
                        ch.close()

        with ExitStack() as c4:
            g = sb("g4", [P, U, CT, HID], ctx=c4)
            ix = sb("ix4", [P, 2, 2 * CT], I32, ctx=c4)
            oh = sb("oh4", [P, 2, CT, W], ctx=c4)
            pA = ps("pA4", [HID, 2, 512], c4)
            ix_in = [sem("ix4_in0"), sem("ix4_in1")]
            g_in = [sem(f"g4_in{u}") for u in range(U)]
            oh_ready = sem("oh4_ready")
            sums_ready = sem("sums4_ready")
            sums_added = sem("sums4_added")
            TURNS = CHUNKS // U
            with nc.Block() as block:
                @block.sync
                def _(e):
                    with e.Fori(0, TURNS) as t:
                        for h in range(2):
                            e.wait_ge(sums_ready, t * U + (2 * h + 2))
                            e.dma_start(ix[:, h, :], src[:, bass.ds(t * (U * CT) + 2 * h * CT, 2 * CT)])\
                                .then_inc(ix_in[h], 16)

                @block.gpsimd
                def _(e):
                    with e.Fori(0, TURNS) as t:
                        for u in range(U):
                            if u % 2 == 0:
                                wait_alone(e, ix_in[u // 2], t * 16 + 16, passed)
                            wait_alone(e, sums_ready, t * U + (u + 1), passed)
                            for j in range(CT):
                                c = (u % 2) * CT + j
                                e.indirect_dma_start(
                                    g[:, u, j, :], None, hs_dram,
                                    bass.IndirectOffsetOnAxis(ap=ix[:, u // 2, c:c + 1], axis=0)
                                ).then_inc(g_in[u], 16)

                @block.tensor
                def _(e):
                    e.sem_inc(sums_ready, U)
                    with e.Fori(0, TURNS) as t:
                        for u in range(U):
                            e.wait_ge(oh_ready, t * U + (u + 1))
                            e.wait_ge(sums_added, t * U + (u + 1))
                            e.wait_ge(g_in[u], t * (16 * CT) + 16 * CT)
                            for j in range(CT):
                                ins = e.matmul(pA[:, u % 2, 0:W], g[:, u, j, :], oh[:, u % 2, j, :],
                                               start=(j == 0), stop=(j == CT - 1))
                            ins.then_inc(sums_ready, 1)

                @block.vector
                def _(e):
                    e.sem_inc(sums_added, 2)

                    def one_hot(to, s):
                        return e.tensor_tensor(
                            to, relf[:, bass.ds(s, 1), :].rearrange("p s (c o) -> p (s c) o", o=1)
                            .to_broadcast((P, CT, W)),
                            k("iota").rearrange("p (o w) -> p o w", o=1).to_broadcast((P, CT, W)),
                            ALU.is_equal)

                    one_hot(oh[:, 0, :, :], FRONT).then_inc(oh_ready, 1)
                    with e.Fori(0, TURNS) as t:
                        for u in range(U):
                            e.wait_ge(sums_ready, t * U + (u + U))
                            one_hot(oh[:, 1 - u % 2, :, :], t * U + (u + FRONT + 1)).then_inc(oh_ready, 1)
                            wk = e.value_load(base_i[0:1, bass.ds(t * U + (u + FRONT), 1)],
                                              min_val=0, max_val=NW - W)
                            e.wait_ge(sums_ready, t * U + (u + U + 1))
                            e.wait_ge(sums_added, t * U + (u + 2))
                            to = gs[0:HID, bass.ds(wk, W)]
                            e.tensor_tensor(to, to, pA[:, u % 2, 0:W], ALU.add).then_inc(sums_added, 1)

        with ExitStack() as c5:
            z = sb("z", [P, 2, GC], ctx=c5)
            ob = sb("ob", [P, 2, GT, D], ctx=c5)
            pZ = ps("pZ", [P, 2, 1024], c5)
            z0_ready = sem("z0_ready")
            z_ready = sem("z_ready")
            y2_ready = sem("y2_ready")
            o_ready = sem("o_ready")
            o_out = [sem("o_out0"), sem("o_out1")]
            o_free = sem("o_free")
            z_one = sem("z_one")
            zf = sb("zf", [HID, 2, GC], ctx=c5)
            with nc.Block() as block:
                @block.sync
                def _(e):
                    e.sem_inc(o_free, 2)
                    with e.Fori(0, GROUPS // 2) as t:
                        for u in range(2):
                            e.wait_ge(o_ready, t * 2 + (u + 1))
                            e.dma_start(og[t * 2 + u], ob[:, u, :, :]).then_inc(o_out[u], 16)
                        for u in range(2):
                            e.wait_ge(o_out[u], t * 16 + 16)
                            e.sem_inc(o_free, 1)
                    e.wait_ge(o_out[0], 16 * (GROUPS // 2))
                    e.wait_ge(o_out[1], 16 * (GROUPS // 2))

                @block.vector
                def _(e):
                    e.memset(z[HID:HID + 32, :, :], 1.0).then_inc(z_one, 1)
                    e.wait_ge(z_one, 1)
                    e.sem_inc(z_ready, 2)
                    with e.Fori(0, GROUPS // 2) as t:
                        for u in range(2):
                            cols = bass.ds((t * 2 + u) * GC, GC)
                            e.wait_ge(z_ready, t * 2 + (u + 1))
                            e.tensor_tensor(zf[:, u, :], gs[0:HID, cols], ac[0:HID, 1, cols], ALU.mult)\
                                .then_inc(z0_ready, 1)
                            e.wait_ge(y2_ready, t * 2 + (u + 1))
                            e.wait_ge(o_free, t * 2 + (u + 1))
                            e.tensor_tensor(ob[:, u, :, :], x2[:, bass.ds((t * 2 + u) * GT, GT), :],
                                            pZ[:, u, 0:GC].rearrange("p (t d) -> p t d", d=D), ALU.add)\
                                .then_inc(o_ready, 1)

                @block.scalar
                def _(e):
                    with e.Fori(0, GROUPS // 2) as t:
                        for u in range(2):
                            e.wait_ge(z0_ready, t * 2 + (u + 1))
                            e.activation(z[0:HID, u, :], zf[:, u, :], ACT.Relu, bias=k("b_conv", HID))\
                                .then_inc(z_ready, 1)

                @block.tensor
                def _(e):
                    e.wait_ge(z_one, 1)
                    with e.Fori(0, GROUPS // 2) as t:
                        for u in range(2):
                            e.wait_ge(z_ready, t * 2 + (u + 3))
                            for j in range(GT):
                                ins = e.matmul(pZ[:, u, j * P:(j + 1) * P], z[0:HID + 1, u, j * P:(j + 1) * P],
                                               k("lin", HID + 1), start=True, stop=True)
                            ins.then_inc(y2_ready, 1)


def kernel(x, src, dst, edge_attr_32, L0_gnn_W_emb, L0_gnn_b_emb, L0_gnn_W_temb, L0_gnn_b_temb,
           L0_gnn_W_tattr, L0_gnn_b_tattr, L0_gnn_W_gate, L0_gnn_b_gate, L0_gnn_W_l, L0_gnn_b_l,
           L0_gnn_W_r, L0_gnn_gamma, L0_gnn_beta, L1_gnn_W_conv, L1_gnn_b_conv, L1_gnn_W_lin,
           L1_gnn_b_lin):
    from concourse import bacc
    from concourse.bass_utils import run_bass_kernel_spmd

    f = np.float32
    x = np.asarray(x)
    src_k = np.zeros((STEPS * EC,), np.int32)
    src_k[0:E] = src
    dst_k = np.full((SLOTS * EC,), N, np.int32)
    dst_k[FRONT * EC:FRONT * EC + E] = dst
    ea_k = np.zeros((SLOTS * EC, EA), f)
    ea_k[FRONT * EC:FRONT * EC + E] = edge_attr_32

    keep = np.zeros((P, KEEP_N), f)
    once = np.zeros((P, ONCE_N), f)

    def put(to, at, name, a, row=0, col=0):
        lo = at[name][0] + col
        a = np.asarray(a)
        to[row:row + a.shape[0], lo:lo + a.shape[1]] = a

    def keeps(*a, **kw):
        put(keep, KEEP_AT, *a, **kw)

    def onces(*a, **kw):
        put(once, ONCE_AT, *a, **kw)

    W_g = np.asarray(L0_gnn_W_gate)
    keeps("W_l", L0_gnn_W_l)
    keeps("W_g1", W_g[0:D])
    keeps("ident", np.eye(P, dtype=f))
    keeps("ones", np.ones((P, P), f))
    keeps("lin", L1_gnn_W_lin)
    keeps("lin", np.asarray(L1_gnn_b_lin)[None, :], row=HID)
    keeps("conv", L1_gnn_W_conv)
    keeps("iota", np.tile(np.arange(W, dtype=f), (P, 1)))
    keeps("b_l", np.asarray(L0_gnn_b_l)[:, None])
    keeps("gamma", np.asarray(L0_gnn_gamma)[:, None])
    keeps("beta", np.asarray(L0_gnn_beta)[:, None])
    keeps("b_conv", np.asarray(L1_gnn_b_conv)[:, None])
    keeps("pmod", (np.arange(P) % W).astype(f)[:, None])
    keeps("eps", np.full((P, 1), EPS, f))
    for c in range(U):
        keeps("emb", L0_gnn_W_emb, row=EA * c, col=EA * c)
        keeps("b_emb", np.asarray(L0_gnn_b_emb)[:, None], row=EA * c)
    onces("AT", np.asarray(L0_gnn_W_tattr).T)
    onces("AT", np.asarray(L0_gnn_W_temb).T, col=EA)
    onces("AT", np.asarray(L0_gnn_b_temb)[:, None], col=ONE)
    onces("BT", np.asarray(L0_gnn_W_tattr).T)
    onces("BT", np.asarray(L0_gnn_b_tattr)[:, None], col=ONE)
    onces("CT", np.asarray(L0_gnn_b_tattr)[:, None], col=ONE)
    onces("e_one", np.ones((1, 1), f), col=ONE)
    onces("W_g2", W_g[D:2 * D])
    onces("W_g3", W_g[2 * D:3 * D])
    onces("W_r", L0_gnn_W_r)
    onces("b_gate", np.asarray(L0_gnn_b_gate)[None, :])

    x_p = np.zeros((NP, D), f)
    x_p[0:N] = x
    arrays = {
        "x": x_p,
        "src": np.ascontiguousarray(src_k.reshape(STEPS, CT, P).transpose(2, 0, 1).reshape(P, -1)),
        "dst": np.ascontiguousarray(dst_k.reshape(SLOTS, CT, P).transpose(2, 0, 1)),
        "dst_row": dst_k.reshape(1, SLOTS, EC),
        "base": np.ascontiguousarray(dst_k[::EC][None, :]),
        "ea": np.ascontiguousarray(ea_k.T).reshape(EA, SLOTS, EC),
        "ea4": np.ascontiguousarray(
            ea_k[(FRONT + 1 - LAG) * EC:(FRONT + 1 - LAG + STEPS + U) * EC].reshape(-1, U, EC, EA)
            .transpose(1, 3, 0, 2).reshape(P, -1, EC)),
        "keep": keep,
        "once": once,
    }
    nc = bacc.Bacc("TRN2", target_bir_lowering=False, num_devices=1)
    args = {n: nc.dram_tensor(n, a.shape, mybir.dt.from_np(a.dtype), kind="ExternalInput").ap()
            for n, a in arrays.items()}
    args["out"] = nc.dram_tensor("out", (NP, D), F32, kind="ExternalOutput").ap()
    gnn_two_layers(nc, **args)
    r = run_bass_kernel_spmd(nc, [arrays], core_ids=[0])
    return r.results[0]["out"][0:N]
```

```python
from contextlib import ExitStack

import numpy as np

import concourse.bass as bass
from concourse import mybir

F32 = mybir.dt.float32
I32 = mybir.dt.int32
BF16 = mybir.dt.bfloat16
ALU = mybir.AluOpType
ACT = mybir.ActivationFunctionType
AX = mybir.AxisListType

P = 128
N = 12500
E = 400000
D = 128
HID = 64
EA, EE = 32, 16
ONE = EA + EE
EPS = 1e-5

W = 64
CT = 4
EC = CT * P
CHUNKS = -(-E // EC) + (-(-E // EC)) % 4
U = 4
LAG = 13
REACH = LAG - 1
STEPS = CHUNKS + 16
FRONT = 16
SLOTS = FRONT + STEPS + 4

NT = -(-N // P)
NP = NT * P
NW = NP + W
GT = 7
GC = GT * P
GROUPS = NT // GT
HALF = GC // 2
BN_PIECE = 500

KEEP = ["W_l", "W_g1", "emb", "ident", "ones", "lin", "conv", "iota", "b_l", "gamma", "beta",
        "b_conv", "pmod", "eps", "b_emb", "spare", "before"]
KEEP_W = [D, D, D, P, P, D, HID, W, 1, 1, 1, 1, 1, 1, 1, 1, P]
ONCE = ["AT", "BT", "CT", "W_g2", "W_g3", "W_r", "e_one", "b_gate", "W_lT"]
ONCE_W = [P, P, P, D, D, D, P, D, P]


def columns(names, widths):
    at, out = 0, {}
    for n, w in zip(names, widths):
        out[n] = (at, at + w)
        at += w
    return out, at


KEEP_AT, KEEP_N = columns(KEEP, KEEP_W)
ONCE_AT, ONCE_N = columns(ONCE, ONCE_W)
assert GROUPS * GT == NT and CHUNKS % U == 0 and STEPS % U == 0 and N % BN_PIECE == 0


def wait_alone(eng, sem, value, passed):
    eng.wait_ge(sem, value)
    eng.sem_inc(passed, 1)


class Chain:

    def __init__(self, eng, sem, turn, per_turn, passed):
        self.eng, self.sem, self.turn, self.per_turn, self.n = eng, sem, turn, per_turn, 0
        self.passed = passed

    def then(self, ins):
        self.n += 1
        ins.then_inc(self.sem, 1)

    def wait(self):
        wait_alone(self.eng, self.sem, self.turn * self.per_turn + self.n, self.passed)

    def close(self):
        assert self.n == self.per_turn, self.n


def gnn_two_layers(nc, x, src, dst, dst_row, base, last, ea, ea4, keep, once, out):
    r_dram = nc.dram_tensor("r_dram", (P, NP), F32).ap()
    rg_dram = nc.dram_tensor("rg_dram", (NW, D), F32).ap()
    h_dram = nc.dram_tensor("h_dram", (NP, 3 * D), BF16).ap()
    hs_dram = nc.dram_tensor("hs_dram", (NP, HID), F32).ap()
    xg = x.rearrange("(g j p) d -> g p j d", j=GT, p=P)
    hg = h_dram.rearrange("(g j p) d -> g p j d", j=GT, p=P)
    hsg = hs_dram.rearrange("(g j p) d -> g p j d", j=GT, p=P)
    rgg = rg_dram[0:NP, :].rearrange("(g j p) d -> g p j d", j=GT, p=P)
    og = out.rearrange("(g j p) d -> g p j d", j=GT, p=P)

    RUN = CHUNKS * EC // P
    dst_cols = dst.rearrange("p s c -> p (s c)")
    ea_cols = ea.rearrange("f s c -> f (s c)")
    rows = dst_row.rearrange("o s c -> o (s c)")

    with ExitStack() as kept:
        def sb(name, shape, dt=F32, ctx=kept):
            return ctx.enter_context(nc.sbuf_tensor(name, shape, dt))

        def ps(name, shape, ctx):
            return ctx.enter_context(nc.psum_tensor(name, shape, F32))

        def sem(name):
            return kept.enter_context(nc.semaphore(name))

        passed = sem("passed")

        ac = sb("ac", [P, 2, NW])
        gs = sb("gs", [P, NW])
        rel = sb("rel", [P, SLOTS, CT], I32)
        relf = rel[:, :, :].bitcast(F32)
        base_p = sb("base_p", [P, SLOTS])
        base_i = sb("base_i", [1, SLOTS], I32)
        kp = sb("kp", [P, KEEP_N])
        wt = sb("wt", [P, 2 * D])

        wlg = sb("wlg", [P, D])

        def k(name, rows=P):
            a, b = KEEP_AT[name]
            return kp[0:rows, a:b]

        flag = sb("flag", [1, 4], I32)
        bn = sb("bn", [P, 8])

        def takes_fast_path(e):
            return e.value_load(flag[0:1, 0:1], min_val=0, max_val=4 * P) == 0

        def general_pass(kind):
            DW = {"sum": 2 * D, "gate": D, "conv": HID}[kind]
            rows_of = {"sum": (h_dram, 3 * D, BF16), "gate": (None, D, F32), "conv": (hs_dram, HID, F32)}[kind]
            acc = nc.dram_tensor(f"acc_{kind}", (NP + P, DW), F32).ap()
            ow_dram = nc.dram_tensor(f"ow_{kind}", (NP, D), F32).ap() if kind == "gate" else None
            table = ow_dram if kind == "gate" else rows_of[0]
            TILES = CHUNKS * CT
            with ExitStack() as c:
                def sbk(name, shape, dt=F32):
                    return sb(f"{name}_{kind}", shape, dt, ctx=c)

                def semk(name):
                    return sem(f"{name}_{kind}")

                got = sbk("got", [P, rows_of[1]], rows_of[2])
                ic = sbk("ic", [P, 1], I32)
                dc = sbk("dc", [P, 1], I32)
                dr = sbk("dr", [P, P], I32)
                dcf = sbk("dcf", [P, 1])
                eq = sbk("eq", [P, P])
                ev = sbk("ev", [P, P])
                ne = sbk("ne", [P, 4])
                to = sbk("to", [P, 1], I32)
                va = sbk("va", [P, DW])
                vs = sbk("vs", [P, DW])
                ft = sbk("ft", [P, P])
                gate = sbk("gate", [P, D])
                pS = ps(f"pS_{kind}", [P, 512], c)
                pF = ps(f"pF_{kind}", [P, 512], c)
                pE = ps(f"pE_{kind}", [P, 512], c)
                zeros_ready, zeros_out = semk("zeros_ready"), semk("zeros_out")
                if kind == "gate":
                    blk_in, blk_ready, blk_out, blk_copied = (semk("blk_in"), semk("blk_ready"),
                                                              semk("blk_out"), semk("blk_copied"))
                    emb_in, emb_ready, feat_ready, pre_ready, gate_ready = (
                        semk("emb_in"), semk("emb_ready"), semk("feat_ready"), semk("pre_ready"),
                        semk("gate_ready"))
                tile_in, got_in, added, tile_free = (semk("tile_in"), semk("got_in"), semk("added"),
                                                     semk("tile_free"))
                to_ready, va_ready, sum_ready, vs_ready = (semk("to_ready"), semk("va_ready"),
                                                           semk("sum_ready"), semk("vs_ready"))
                acc_in, turned, merged = semk("acc_in"), semk("turned"), semk("merged")
                chain = semk("chain")
                LOADS = 4 if kind == "gate" else 3
                with nc.Block() as block:
                    @block.sync
                    def _(e):
                        with e.If(takes_fast_path(e)):
                            pass
                        with e.Else():
                            e.wait_ge(zeros_ready, 1)
                            with e.Fori(0, NT + 1) as t:
                                e.dma_start(acc[bass.ds(t * P, P), :], va[:, :]).then_inc(zeros_out, 16)
                            e.wait_ge(zeros_out, 16 * (NT + 1))
                            e.sem_inc(tile_free, 1)
                            if kind == "gate":
                                with e.Fori(0, NT) as t:
                                    wait_alone(e, blk_copied, t + 1, passed)
                                    e.dma_start(ow_dram[bass.ds(t * P, P), :], gate[:, :]).then_inc(blk_out, 16)
                                    e.wait_ge(blk_out, t * 16 + 16)
                                    e.sem_inc(blk_in, 1)
                            with e.Fori(0, TILES) as t:
                                wait_alone(e, tile_free, t + 1, passed)
                                if kind == "gate":
                                    e.dma_start(ic[:, :], dst_cols[:, bass.ds(t + FRONT * CT, 1)],
                                                allow_slow_non_contiguous=True)\
                                        .then_inc(tile_in, 16)
                                    e.dma_start(ft[0:EA, :], ea_cols[:, bass.ds(t * P + FRONT * EC, P)])\
                                        .then_inc(tile_in, 16)
                                else:
                                    e.dma_start(ic[:, :], src[:, bass.ds(t, 1)], allow_slow_non_contiguous=True).then_inc(tile_in, 16)
                                e.dma_start(dc[:, :], dst_cols[:, bass.ds(t + FRONT * CT, 1)],
                                            allow_slow_non_contiguous=True).then_inc(tile_in, 16)
                                e.dma_start(dr[:, :], rows[:, bass.ds(t * P + FRONT * EC, P)]
                                            .to_broadcast((P, P))).then_inc(tile_in, 16)
                            e.wait_ge(tile_free, TILES + 1)
                            with e.Fori(0, NT) as t:
                                wait_alone(e, merged, t + 1, passed)
                                e.dma_start(vs[:, :], acc[bass.ds(t * P, P), :]).then_inc(acc_in, 16)

                    @block.gpsimd
                    def _(e):
                        with e.If(takes_fast_path(e)):
                            pass
                        with e.Else():
                            if kind == "gate":
                                e.wait_ge(blk_in, NT + 1)
                            with e.Fori(0, TILES) as t:
                                wait_alone(e, tile_in, t * (16 * LOADS) + 16 * LOADS, passed)
                                e.indirect_dma_start(got[:, :], None, table,
                                                     bass.IndirectOffsetOnAxis(ap=ic[:, 0:1], axis=0))\
                                    .then_inc(got_in, 16)
                                wait_alone(e, to_ready, t + 1, passed)
                                wait_alone(e, vs_ready, t + 1, passed)
                                e.indirect_dma_start(acc, bass.IndirectOffsetOnAxis(ap=to[:, 0:1], axis=0),
                                                     vs[:, :], None, compute_op=ALU.add).then_inc(added, 16)
                                e.wait_ge(added, t * 16 + 16)
                                e.sem_inc(tile_free, 1)

                    @block.tensor
                    def _(e):
                        with e.If(takes_fast_path(e)):
                            pass
                        with e.Else():
                            if kind == "gate":
                                with e.Fori(0, NT) as t:
                                    e.wait_ge(blk_ready, t + 1)
                                    e.matmul(pS[:, 0:D], eq[:, :], k("W_g1"), start=True, stop=True)\
                                        .then_inc(turned, 1)
                            with e.Fori(0, TILES) as t:
                                if kind == "gate":
                                    wait_alone(e, tile_in, t * (16 * LOADS) + 16 * LOADS, passed)
                                    e.matmul(pE[0:EE, 0:P], k("emb")[0:EA, 0:EE], ft[0:EA, :],
                                             start=True, stop=True).then_inc(emb_in, 1)
                                    e.wait_ge(emb_ready, t + 1)
                                    e.matmul(pF[:, 0:2 * D], ft[0:64, :], wt[0:64, :], start=True, stop=True)\
                                        .then_inc(feat_ready, 1)
                                e.wait_ge(to_ready, t + 1)
                                e.wait_ge(va_ready, t + 1)
                                e.matmul(pS[:, 0:DW], eq[:, :], va[:, :], start=True, stop=True)\
                                    .then_inc(sum_ready, 1)
                            with e.Fori(0, NT) as t:
                                wait_alone(e, acc_in, t * 16 + 16, passed)
                                for b in range(2 if kind == "sum" else 1):
                                    ins = e.transpose(pS[0:min(DW, P), b * P:(b + 1) * P],
                                                      vs[:, b * P:min(DW, (b + 1) * P)], k("ident"))
                                ins.then_inc(turned, 1)

                    @block.scalar
                    def _(e):
                        with e.If(takes_fast_path(e)):
                            pass
                        with e.Else():
                            if kind == "gate":
                                e.wait_ge(zeros_ready, 1)
                                with e.Fori(0, TILES) as t:
                                    e.wait_ge(emb_in, t + 1)
                                    e.activation(ft[EA:ONE, :], pE[0:EE, 0:P], ACT.Relu,
                                                 bias=k("b_emb")[0:EE, :]).then_inc(emb_ready, 1)
                                    e.wait_ge(pre_ready, t + 1)
                                    e.activation(gate[:, :], gate[:, :], ACT.Sigmoid).then_inc(gate_ready, 1)

                    @block.vector
                    def _(e):
                        with e.If(takes_fast_path(e)):
                            pass
                        with e.Else():
                            e.memset(ft[:, :], 1.0)
                            e.memset(va[:, :], 0.0).then_inc(zeros_ready, 1)
                            e.sem_inc(merged, 1)
                            e.wait_ge(zeros_out, 16 * (NT + 1))
                            if kind == "sum":
                                e.memset(va[:, :], 1.0)
                            if kind == "gate":
                                e.sem_inc(blk_in, 1)
                                with e.Fori(0, NT) as t:
                                    e.wait_ge(blk_in, t + 1)
                                    e.tensor_copy(eq[:, :], gs[:, bass.ds(t * P, P)]).then_inc(blk_ready, 1)
                                    e.wait_ge(turned, t + 1)
                                    e.tensor_copy(gate[:, :], pS[:, 0:D]).then_inc(blk_copied, 1)
                            PER = {"sum": 7, "gate": 6, "conv": 6}[kind]
                            with e.Fori(0, TILES) as t:
                                ch = Chain(e, chain, t, PER, passed)
                                wait_alone(e, tile_in, t * (16 * LOADS) + 16 * LOADS, passed)
                                ch.then(e.tensor_copy(dcf[:, :], dc[:, :]))
                                ch.wait()
                                ch.then(e.tensor_scalar(eq[:, :], dr[:, :], dcf[:, 0:1], None, ALU.is_equal))
                                ch.wait()
                                ch.then(e.tensor_tensor(ev[:, :], eq[:, :], k("before"), ALU.mult))
                                ch.wait()
                                ch.then(e.tensor_reduce(ne[:, 0:1], ev[:, :], AX.X, ALU.max))
                                ch.then(e.tensor_tensor(ne[:, 1:2], k("spare"), dcf[:, :], ALU.subtract))
                                ch.wait()
                                ch.then(e.tensor_tensor(ne[:, 2:3], ne[:, 1:2], ne[:, 0:1], ALU.mult))
                                ch.wait()
                                e.tensor_tensor(to[:, :], ne[:, 2:3], dcf[:, :], ALU.add).then_inc(to_ready, 1)
                                e.wait_ge(got_in, t * 16 + 16)
                                if kind == "sum":
                                    ch.then(e.tensor_tensor(ev[:, :], got[:, D:2 * D], got[:, 2 * D:3 * D], ALU.add))
                                    ch.wait()
                                    e.tensor_tensor(va[:, 0:D], ev[:, :], got[:, 0:D], ALU.add)\
                                        .then_inc(va_ready, 1)
                                elif kind == "gate":
                                    e.wait_ge(feat_ready, t + 1)
                                    e.tensor_tensor(gate[:, :], got[:, :], pF[:, 0:D], ALU.add)\
                                        .then_inc(pre_ready, 1)
                                    e.wait_ge(gate_ready, t + 1)
                                    e.tensor_tensor(va[:, :], gate[:, :], pF[:, D:2 * D], ALU.mult)\
                                        .then_inc(va_ready, 1)
                                else:
                                    e.tensor_copy(va[:, :], got[:, :]).then_inc(va_ready, 1)
                                e.wait_ge(sum_ready, t + 1)
                                e.tensor_copy(vs[:, :], pS[:, 0:DW]).then_inc(vs_ready, 1)
                                ch.close()
                            e.wait_ge(tile_free, TILES + 1)
                            with e.Fori(0, NT) as t:
                                e.wait_ge(turned, t + (NT + 1 if kind == "gate" else 1))
                                cols = bass.ds(t * P, P)
                                if kind == "sum":
                                    e.tensor_copy(ac[:, :, cols], pS[:, 0:2 * P]
                                                  .rearrange("p (a c) -> p a c", a=2)).then_inc(merged, 1)
                                else:
                                    e.tensor_tensor(gs[0:DW, cols], gs[0:DW, cols], pS[0:DW, 0:P], ALU.add)\
                                        .then_inc(merged, 1)

        with ExitStack() as c0:
            xb = sb("x0", [P, 2, GT, D], ctx=c0)
            hb = sb("h0", [P, GT, D], ctx=c0)
            hr = sb("hr0", [P, GT, D], ctx=c0)
            hp = sb("hp0", [P, GT, 3 * D], BF16, ctx=c0)
            hT = sb("hT0", [P, GC], ctx=c0)
            rT = sb("rT0", [P, GC], ctx=c0)
            st = sb("st0", [P, GT, 6], ctx=c0)
            mv = sb("mv0", [P, GT, 2], ctx=c0)
            rs = sb("rs0", [P, GT], ctx=c0)
            nb = sb("nb0", [P, GT], ctx=c0)
            sd = sb("sd0", [P, GT], ctx=c0)
            rgb = sb("rg0", [P, GT, D], ctx=c0)
            zero = sb("zero0", [W, D], ctx=c0)
            on = gs[:, 0:ONCE_N]
            at = ONCE_N
            baseb = gs[:, at:at + SLOTS].bitcast(I32)
            lastb = gs[:, at + SLOTS:at + 2 * SLOTS].bitcast(I32)
            at += 2 * SLOTS
            cur = gs[:, at:at + RUN]
            nxt = gs[:, at + RUN:at + 2 * RUN]
            vm = sb("vm", [P, 4], ctx=c0)
            vf = sb("vf", [P, 4], ctx=c0)
            fl = sb("fl", [1, 1], ctx=c0)
            pV = ps("pV", [P, 512], c0)
            viol_ready = sem("viol_ready")
            viol_sum = sem("viol_sum")
            flags = sem("flags")
            pT = ps("pT0", [P, 1024], c0)
            pR = ps("pR0", [P, 1024], c0)
            pW = ps("pW0", [P, 512], c0)
            pN = ps("pN0", [P, 1024], c0)

            def o(name, rows=P):
                a, b = ONCE_AT[name]
                return on[0:rows, a:b]

            consts_in = sem("consts_in")
            tables_in = sem("tables_in")
            x_in = [sem("x_in0"), sem("x_in1")]
            h_out = sem("h_out")
            hi_ready = sem("hi_ready")
            rest_ready = sem("rest_ready")
            mid_ready = sem("mid_ready")
            lo_ready = sem("lo_ready")
            ones_ready = sem("ones_ready")
            h_free = sem("h_free")
            rT_free = sem("rT_free")
            rg_ready = sem("rg_ready")
            rg_copied = sem("rg_copied")
            rg_out = sem("rg_out")
            r_out = sem("r_out")
            pad_out = sem("pad_out")
            chain0 = sem("chain0")
            stats_ready = sem("stats_ready")
            std_ready = sem("std_ready")
            ready_stats = sem("ready_stats")
            ready_h = sem("ready_h")
            ready_hT = sem("ready_hT")
            hT_copied = sem("hT_copied")
            ready_r = sem("ready_r")
            ready_rT = sem("ready_rT")
            ready_wt = sem("ready_wt")
            zeroed = sem("zeroed")
            setup = sem("setup")
            T0 = GROUPS // 2
            with nc.Block() as block:
                @block.sync
                def _(e):
                    e.dma_start(kp[:, :], keep).then_inc(consts_in, 16)
                    e.dma_start(on, once).then_inc(consts_in, 16)
                    e.dma_start(rel[:, :, :], dst).then_inc(tables_in, 16)
                    e.dma_start(base_i[:, :], base).then_inc(tables_in, 16)
                    e.dma_start(baseb, base.to_broadcast((P, SLOTS))).then_inc(tables_in, 16)
                    e.dma_start(lastb, last.to_broadcast((P, SLOTS))).then_inc(tables_in, 16)
                    for to, first in ((cur, FRONT * EC), (nxt, FRONT * EC + 1)):
                        e.dma_start(to.bitcast(I32), rows[:, first:first + P * RUN]
                                    .rearrange("o (p c) -> (o p) c", p=P)).then_inc(tables_in, 16)
                    with e.Fori(0, T0) as t:
                        for u in range(2):
                            e.wait_ge(ready_h, t * 2 + (u + 1))
                            e.dma_start(xb[:, u, :, :], xg[t * 2 + u]).then_inc(x_in[u], 16)

                @block.gpsimd
                def _(e):
                    e.sem_inc(h_free, 1)
                    e.sem_inc(rT_free, 1)
                    e.memset(zero[:, :], 0.0).then_inc(zeroed, 1)
                    e.memset(ac[:, :, :], 0.0).then_inc(zeroed, 1)
                    e.wait_ge(zeroed, 2)
                    e.dma_start(rg_dram[NP:NW, :], zero[:, :]).then_inc(pad_out, 16)
                    e.wait_ge(pad_out, 16)
                    with e.Fori(0, T0) as t:
                        for u in range(2):
                            e.wait_ge(hi_ready, t * 2 + (u + 1))
                            e.tensor_tensor(hr[:, :, :], hb[:, :, :], hp[:, :, 0:D], ALU.subtract)\
                                .then_inc(rest_ready, 1)
                            e.wait_ge(lo_ready, t * 2 + (u + 1))
                            e.dma_start(hg[t * 2 + u], hp[:, :, :]).then_inc(h_out, 16)
                            e.wait_ge(ready_rT, t * 2 + (u + 1))
                            e.dma_start(r_dram[:, bass.ds((t * 2 + u) * GC, GC)], rT[:, :]).then_inc(r_out, 16)
                            e.wait_ge(rg_copied, t * 2 + (u + 1))
                            e.dma_start(rgg[t * 2 + u], rgb[:, :, :]).then_inc(rg_out, 16)
                            e.wait_ge(rg_out, t * 32 + (16 * u + 16))
                            e.wait_ge(h_out, t * 32 + (16 * u + 16))
                            e.sem_inc(h_free, 1)
                            e.wait_ge(r_out, t * 32 + (16 * u + 16))
                            e.sem_inc(rT_free, 1)

                @block.vector
                def _(e):
                    e.sem_inc(ready_h, 2)
                    e.wait_ge(tables_in, 96)
                    e.tensor_tensor(relf, rel[:, :, :],
                                    baseb.rearrange("p (s o) -> p s o", o=1).to_broadcast((P, SLOTS, CT)),
                                    ALU.subtract).then_inc(setup, 1)
                    e.wait_ge(consts_in, 32)
                    e.tensor_scalar(base_p[:, :], baseb, k("pmod"), None, ALU.add).then_inc(setup, 1)
                    real = slice(FRONT, FRONT + CHUNKS)
                    e.tensor_tensor(cur, nxt.bitcast(I32), cur.bitcast(I32), ALU.subtract).then_inc(flags, 1)
                    ahead = lastb[:, FRONT:FRONT + CHUNKS - REACH]
                    e.tensor_tensor(ahead.bitcast(F32), baseb[:, FRONT + REACH:FRONT + CHUNKS], ahead,
                                    ALU.subtract).then_inc(flags, 1)
                    e.wait_ge(setup, 1)
                    e.wait_ge(flags, 2)
                    e.tensor_reduce(vm[:, 0:1], cur, AX.X, ALU.min).then_inc(flags, 1)
                    e.tensor_reduce(vm[:, 1:2], relf[:, real, :], AX.XY, ALU.min).then_inc(flags, 1)
                    e.tensor_reduce(vm[:, 2:3], relf[:, real, :], AX.XY, ALU.max).then_inc(flags, 1)
                    e.tensor_reduce(vm[:, 3:4], ahead.bitcast(F32), AX.X, ALU.min).then_inc(flags, 1)
                    e.wait_ge(flags, 6)
                    e.tensor_scalar(vf[:, 0:2], vm[:, 0:2], 0.0, None, ALU.is_lt).then_inc(viol_ready, 1)
                    e.tensor_scalar(vf[:, 2:3], vm[:, 2:3], float(W), None, ALU.is_ge).then_inc(viol_ready, 1)
                    e.tensor_scalar(vf[:, 3:4], vm[:, 3:4], 1.0, None, ALU.is_lt).then_inc(viol_ready, 1)
                    e.wait_ge(viol_sum, 1)
                    e.tensor_reduce(fl[:, :], pV[0:1, 0:4], AX.X, ALU.add).then_inc(flags, 1)
                    e.wait_ge(flags, 7)
                    e.tensor_copy(flag[:, 0:1], fl[:, :]).then_inc(setup, 1)
                    e.wait_ge(ready_wt, 1)
                    e.tensor_copy(wt[:, :], pW[:, 0:2 * D]).then_inc(setup, 1)
                    e.tensor_copy(wlg[:, :], pW[:, 2 * D:3 * D]).then_inc(setup, 1)
                    with e.Fori(0, T0) as t:
                        ch = Chain(e, chain0, t, 6, passed)
                        for u in range(2):
                            wait_alone(e, x_in[u], t * 16 + 16, passed)
                            for j in range(GT):
                                ins = e.bn_stats(st[:, j, :], xb[:, u, j, :])
                            ch.then(ins)
                            ch.wait()
                            wait_alone(e, ready_h, t * 2 + (u + 2), passed)
                            for j in range(GT):
                                ins = e.bn_aggr(mv[:, j, :], st[:, j, :])
                            ch.then(ins)
                            ch.wait()
                            e.sem_inc(stats_ready, 1)
                            e.wait_ge(std_ready, t * 2 + (u + 1))
                            ch.then(e.reciprocal(rs[:, :], sd[:, :]))
                            ch.wait()
                            e.scalar_tensor_tensor(out=nb[:, :], in0=mv[:, :, 0], scalar=-1.0,
                                                   in1=rs[:, :], op0=ALU.mult, op1=ALU.mult)\
                                .then_inc(ready_stats, 1)
                            e.wait_ge(mid_ready, t * 2 + (u + 1))
                            e.tensor_tensor(hp[:, :, 2 * D:3 * D], hr[:, :, :], hp[:, :, D:2 * D],
                                            ALU.subtract).then_inc(lo_ready, 1)
                            e.wait_ge(ready_hT, t * 2 + (u + 1))
                            e.tensor_copy(hT[:, :], pT[:, 0:GC]).then_inc(hT_copied, 1)
                            e.wait_ge(ready_r, t * 2 + (u + 1))
                            e.wait_ge(rT_free, t * 2 + (u + 1))
                            e.tensor_scalar(rT[:, :].rearrange("p (a b) -> p a b", a=2),
                                            pR[:, :].rearrange("p (a b) -> p a b", a=2)[:, :, 0:HALF],
                                            k("b_l"), None, ALU.add).then_inc(ready_rT, 1)
                        ch.close()
                    e.wait_ge(ready_r, GROUPS)
                    e.memset(gs[:, :], 0.0).then_inc(setup, 1)
                    e.wait_ge(setup, 6)

                @block.scalar
                def _(e):
                    with e.Fori(0, T0) as t:
                        for u in range(2):
                            e.wait_ge(stats_ready, t * 2 + (u + 1))
                            e.activation(sd[:, :], mv[:, :, 1], ACT.Sqrt, bias=k("eps"))\
                                .then_inc(std_ready, 1)
                            e.wait_ge(ready_stats, t * 2 + (u + 1))
                            e.wait_ge(h_free, t * 2 + (u + 1))
                            e.wait_ge(hT_copied, t * 2 + (u + 1))
                            for j in range(GT):
                                ins = e.activation(hb[:, j, :], xb[:, u, j, :], ACT.Relu,
                                                   bias=nb[:, j:j + 1], scale=rs[:, j:j + 1])
                            ins.then_inc(ready_h, 1)
                            e.wait_ge(ready_h, t * 2 + (u + 3))
                            e.activation(hp[:, :, 0:D], hb[:, :, :], ACT.Copy).then_inc(hi_ready, 1)
                            e.wait_ge(rest_ready, t * 2 + (u + 1))
                            e.activation(hp[:, :, D:2 * D], hr[:, :, :], ACT.Copy).then_inc(mid_ready, 1)
                            e.wait_ge(rg_ready, t * 2 + (u + 1))
                            e.activation(rgb[:, :, :], pN[:, 0:GC].rearrange("p (t d) -> p t d", d=D), ACT.Copy)\
                                .then_inc(rg_copied, 1)

                @block.tensor
                def _(e):
                    e.sem_inc(hT_copied, 1)
                    e.wait_ge(consts_in, 32)
                    e.matmul(pW[:, D:2 * D], o("AT"), k("ident"), start=True, stop=False)
                    e.matmul(pW[:, D:2 * D], o("CT"), k("ident"), start=False, stop=True)
                    e.matmul(pW[:, 0:D], o("AT"), o("W_g2"), start=True, stop=False)
                    e.matmul(pW[:, 0:D], o("CT"), o("W_g2"), start=False, stop=False)
                    e.matmul(pW[:, 0:D], o("BT"), o("W_g3"), start=False, stop=False)
                    e.matmul(pW[:, 0:D], o("e_one"), o("b_gate"), start=False, stop=True)
                    e.matmul(pW[:, 2 * D:3 * D], o("W_lT"), k("W_g1"), start=True, stop=True).then_inc(ready_wt, 1)
                    e.wait_ge(viol_ready, 3)
                    e.matmul(pV[:, 0:4], k("ones"), vf[:, :], start=True, stop=True).then_inc(viol_sum, 1)
                    with e.Fori(0, T0) as t:
                        for u in range(2):
                            e.wait_ge(ready_h, t * 2 + (u + 3))
                            for j in range(GT):
                                ins = e.transpose(pT[:, j * P:(j + 1) * P], hb[:, j, :], k("ident"))
                            ins.then_inc(ready_hT, 1)
                            e.wait_ge(hT_copied, t * 2 + (u + 2))
                            for b in range(2):
                                ins = e.matmul(pR[:, b * 512:b * 512 + HALF], o("W_r"),
                                               hT[:, b * HALF:(b + 1) * HALF], start=True, stop=True)
                            ins.then_inc(ready_r, 1)
                            e.wait_ge(ready_rT, t * 2 + (u + 1))
                            e.wait_ge(rg_copied, t * 2 + u)
                            for j in range(GT):
                                ins = e.matmul(pN[:, j * P:(j + 1) * P], rT[:, j * P:(j + 1) * P], k("W_g1"),
                                               start=True, stop=True)
                            ins.then_inc(rg_ready, 1)

        with ExitStack() as c1:
            g = sb("g", [P, U, CT, 3 * D], BF16, ctx=c1)
            ix = sb("ix", [P, 2, 2 * CT], I32, ctx=c1)
            oh1 = sb("oh1", [P, 2, CT, W], BF16, ctx=c1)
            oh2 = sb("oh2", [P, 2, CT, W], ctx=c1)
            fs = sb("fs", [P, U, EC], ctx=c1)
            e4 = sb("e4", [P, EC], ctx=c1)
            onesb = sb("onesb", [P, P], BF16, ctx=c1)
            rw = sb("rw", [P, 2, 2, D], ctx=c1)
            ag = sb("ag", [P, 2, P], ctx=c1)
            rc = sb("rc", [P, 2], ctx=c1)
            gm = sb("gm", [P, 2, CT, D], ctx=c1)
            pF = ps("pF", [P, 2, CT, 2, D], c1)
            pA = ps("pA", [P, 512], c1)
            pE = ps("pE", [P, 512], c1)
            pG = ps("pG", [P, 512], c1)
            pM = ps("pM", [P, 512], c1)

            ix_in = [sem("ix_in0"), sem("ix_in1")]
            g_in = [sem(f"g_in{u}") for u in range(U)]
            ea_in = [sem("ea_in0"), sem("ea_in1")]
            db_in = [sem("db_in0"), sem("db_in1")]
            e4_in = sem("e4_in")
            rw_in = [sem("rw_in0"), sem("rw_in1")]
            oh1_ready = sem("oh1_ready")
            sums_ready = sem("sums_ready")
            sums_added = sem("sums_added")
            emb_in = sem("emb_in")
            emb_ready = sem("emb_ready")
            ag_ready = sem("ag_ready")
            gw_in = sem("gw_in")
            gw_ready = sem("gw_ready")
            ohT_ready = sem("ohT_ready")
            oh2_ready = sem("oh2_ready")
            feat_ready = sem("feat_ready")
            gate_ready = sem("gate_ready")
            msg_ready = sem("msg_ready")
            gsum_ready = sem("gsum_ready")
            gsum_added = sem("gsum_added")
            chain1 = sem("chain1")
            cleared = sem("cleared")
            CLEARS = 5
            TURNS = STEPS // U

            def slot(t, u, shift):
                return t * U + (u + FRONT + shift)

            def load_ix(e, h, t):
                e.dma_start(ix[:, h, :], src[:, bass.ds(t * (U * CT) + 2 * h * CT, 2 * CT)])\
                    .then_inc(ix_in[h], 16)

            def load_bases(e, s, n):
                return nc.values_load_multi_w_load_instructions(
                    base_i[0:1, bass.ds(s, n)], engines=[e.engine], min_val=0, max_val=NW - W)[1]

            with nc.Block() as block:
                @block.sync
                def _(e):
                    with e.If(takes_fast_path(e)):
                        e.wait_ge(cleared, CLEARS)
                        load_ix(e, 0, 0)
                        e.dma_start(e4[:, :], ea4[:, 0, :]).then_inc(e4_in, 16)
                        with e.Fori(0, TURNS) as t:
                            for h in range(2):
                                s0 = slot(t, 2 * h, 1 - LAG)
                                e.wait_ge(gw_ready, t * U + (2 * h + 2))
                                for v, first in enumerate(load_bases(e, slot(t, 2 * h, 1 - LAG), 2)):
                                    e.dma_start(rw[64:64 + W, h, v, :], rg_dram[bass.ds(first, W), :])\
                                        .then_inc(rw_in[h], 16)
                                e.wait_ge(feat_ready, t * U + (2 * h + 3))
                                e.dma_start(fs[0:EA, 2 * h:2 * h + 2, :], ea[:, bass.ds(s0, 2), :])\
                                    .then_inc(ea_in[h], 16)
                                e.dma_start(fs[64:64 + W, 2 * h:2 * h + 2, :].bitcast(I32),
                                            dst_row[0:1, bass.ds(s0, 2), :].to_broadcast((W, 2, EC)))\
                                    .then_inc(db_in[h], 16)
                                if h == 1:
                                    e.wait_ge(emb_in, t + 1)
                                    e.dma_start(e4[:, :], ea4[:, bass.ds(t + 1, 1), :]
                                                .rearrange("p o c -> p (o c)")).then_inc(e4_in, 16)
                                other = 2 * (1 - h)
                                e.wait_ge(g_in[other], (t + h) * (16 * CT))
                                e.wait_ge(g_in[other + 1], (t + h) * (16 * CT))
                                load_ix(e, 1 - h, t + h)
                        e.wait_ge(ix_in[0], 16 * TURNS + 16)
                        e.wait_ge(ix_in[1], 16 * TURNS)
                        e.wait_ge(e4_in, 16 * TURNS + 16)

                @block.gpsimd
                def _(e):
                    with e.If(takes_fast_path(e)):
                        with e.Fori(0, TURNS) as t:
                            for u in range(U):
                                if u % 2 == 0:
                                    wait_alone(e, ix_in[u // 2], t * 16 + 16, passed)
                                wait_alone(e, sums_ready, t * U + (u + 1), passed)
                                for j in range(CT):
                                    c = (u % 2) * CT + j
                                    e.indirect_dma_start(
                                        g[:, u, j, :], None, h_dram,
                                        bass.IndirectOffsetOnAxis(ap=ix[:, u // 2, c:c + 1], axis=0)
                                    ).then_inc(g_in[u], 16)

                @block.tensor
                def _(e):
                    with e.If(takes_fast_path(e)):
                        e.sem_inc(sums_ready, U)
                        e.sem_inc(feat_ready, U)
                        e.sem_inc(gsum_ready, 1)
                        e.wait_ge(cleared, CLEARS)
                        with e.Fori(0, TURNS) as t:
                            for u in range(U):
                                b, h, v = u % 2, u // 2, u % 2
                                e.wait_ge(oh1_ready, t * U + (u + 1))
                                e.wait_ge(sums_added, t * U + (u + 1))
                                e.wait_ge(g_in[u], t * (16 * CT) + 16 * CT)
                                for j in range(CT):
                                    for part in range(3):
                                        e.matmul(pA[:, 0:W], g[:, u, j, part * D:(part + 1) * D], oh1[:, b, j, :],
                                                 start=(j == 0 and part == 0), stop=(j == CT - 1 and part == 2))
                                for j in range(CT):
                                    ins = e.matmul(pA[:, W:2 * W], onesb[:, :], oh1[:, b, j, :],
                                                   start=(j == 0), stop=(j == CT - 1))
                                ins.then_inc(sums_ready, 1)
                                e.wait_ge(emb_ready, t * U + (u + 1))
                                e.wait_ge(gw_ready, t * U + (u + U))
                                e.wait_ge(ohT_ready, t * U + (u + 1))
                                for j in range(CT):
                                    ins = e.matmul(pF[:, b, j, :, :].rearrange("p a d -> p (a d)"),
                                                   fs[:, (u - 1) % U, j * P:(j + 1) * P], wt[:, :],
                                                   start=True, stop=True)
                                ins.then_inc(feat_ready, 1)
                                if u == 0:
                                    wait_alone(e, e4_in, t * 16 + 16, passed)
                                    e.matmul(pE[:, :], k("emb"), e4[:, :], start=True, stop=True)\
                                        .then_inc(emb_in, 1)
                                e.wait_ge(ag_ready, t * U + (u + 1))
                                e.matmul(pG[:, 0:D], ag[:, 0, :], wlg[:, :], start=True, stop=True)
                                e.matmul(pG[:, D:D + 1], ag[0:1, 1, :], k("ones", 1)[:, 0:1],
                                         start=True, stop=True).then_inc(gw_in, 1)
                                e.wait_ge(msg_ready, t * U + (u + 1))
                                e.wait_ge(oh2_ready, t * U + (u + 1))
                                e.wait_ge(gsum_added, t * U + (u + 1))
                                for j in range(CT):
                                    ins = e.matmul(pM[:, 0:W],
                                                   gm[:, 1 - b, j, :], oh2[:, 1 - b, j, :],
                                                   start=(j == 0), stop=(j == CT - 1))
                                ins.then_inc(gsum_ready, 1)

                @block.scalar
                def _(e):
                    with e.If(takes_fast_path(e)):
                        e.wait_ge(cleared, CLEARS)
                        e.sem_inc(emb_ready, 1)
                        with e.Fori(0, TURNS) as t:
                            w_a = load_bases(e, slot(t, 0, 1 - LAG), U)
                            for u in range(U):
                                b, h = u % 2, u // 2
                                e.wait_ge(sums_added, t * U + (u + 1))
                                e.wait_ge(gw_in, t * U + u)
                                e.activation(ag[:, :, W:2 * W], ac[:, :, bass.ds(w_a[u], W)], ACT.Copy)\
                                    .then_inc(ag_ready, 1)
                                e.wait_ge(feat_ready, t * U + (u + U + 1))
                                e.wait_ge(gsum_ready, t * U + (u + 1))
                                e.activation(gm[:, b, :, :], pF[:, b, :, 0, :], ACT.Sigmoid).then_inc(gate_ready, 1)
                                e.wait_ge(emb_in, t + 1)
                                e.wait_ge(ea_in[h], t * 16 + 16)
                                e.activation(fs[EA:ONE, u, :], pE[EA * u:EA * u + EE, :], ACT.Relu,
                                             bias=k("b_emb")[EA * u:EA * u + EE, :]).then_inc(emb_ready, 1)

                @block.vector
                def _(e):
                    with e.If(takes_fast_path(e)):
                        e.memset(fs[:, :, :], 1.0).then_inc(cleared, 1)
                        e.memset(onesb[:, :], 1.0).then_inc(cleared, 1)
                        e.memset(ag[:, :, :], 0.0).then_inc(cleared, 1)
                        e.memset(gm[:, :, :, :], 0.0).then_inc(cleared, 1)
                        e.memset(oh2[:, :, :, :], 0.0).then_inc(cleared, 1)
                        e.wait_ge(cleared, CLEARS)
                        e.sem_inc(sums_added, 1)
                        e.sem_inc(gsum_added, 1)
                        e.sem_inc(ohT_ready, 1)
                        e.sem_inc(gw_ready, U)
                        e.sem_inc(msg_ready, 1)
                        e.sem_inc(oh2_ready, 1)

                        def one_hot(to, s):
                            return e.tensor_tensor(
                                to, relf[:, bass.ds(s, 1), :].rearrange("p s (c o) -> p (s c) o", o=1)
                                .to_broadcast((P, CT, W)),
                                k("iota").rearrange("p (o w) -> p o w", o=1).to_broadcast((P, CT, W)),
                                ALU.is_equal)

                        one_hot(oh1[:, 0, :, :], FRONT).then_inc(oh1_ready, 1)
                        with e.Fori(0, TURNS) as t:
                            ch = Chain(e, chain1, t, 2 * U, passed)
                            w_k = load_bases(e, slot(t, 0, 0), U)
                            w_g = load_bases(e, slot(t, 0, -1 - LAG), U)
                            for u in range(U):
                                b, h, v = u % 2, u // 2, u % 2
                                e.wait_ge(gsum_ready, t * U + (u + 1))
                                one_hot(oh2[:, b, :, :], slot(t, u, -LAG)).then_inc(oh2_ready, 1)
                                wk = w_k[u]
                                e.wait_ge(sums_ready, t * U + (u + U + 1))
                                e.wait_ge(sums_added, t * U + (u + 1))
                                e.wait_ge(ag_ready, t * U + (u + 1))
                                to = ac[:, :, bass.ds(wk, W)]
                                e.tensor_tensor(to, to, pA[:, 0:2 * W].rearrange("p (a w) -> p a w", a=2),
                                                ALU.add).then_inc(sums_added, 1)
                                one_hot(oh1[:, 1 - b, :, :], slot(t, u, 1)).then_inc(oh1_ready, 1)
                                e.wait_ge(gw_in, t * U + (u + 1))
                                ch.then(e.tensor_scalar(rc[64:P, 0:1], pG[64:P, D:D + 1], 1.0, None, ALU.max))
                                ch.wait()
                                ch.then(e.reciprocal(rc[64:P, 1:2], rc[64:P, 0:1]))
                                e.wait_ge(rw_in[h], t * 32 + 32)
                                ch.wait()
                                e.scalar_tensor_tensor(out=wt[64:P, 0:D], in0=pG[64:P, 0:D], scalar=rc[64:P, 1:2],
                                                       in1=rw[64:P, h, v, :], op0=ALU.mult, op1=ALU.add)\
                                    .then_inc(gw_ready, 1)
                                e.wait_ge(db_in[h], t * 16 + 16)
                                e.tensor_scalar(fs[64:64 + W, u, :], fs[64:64 + W, u, :].bitcast(I32),
                                                base_p[64:64 + W, bass.ds(slot(t, u, 1 - LAG), 1)], None,
                                                ALU.is_equal).then_inc(ohT_ready, 1)
                                e.wait_ge(gate_ready, t * U + (u + 1))
                                e.tensor_tensor(gm[:, b, :, :], gm[:, b, :, :], pF[:, b, :, 1, :],
                                                ALU.mult).then_inc(msg_ready, 1)
                                e.wait_ge(gsum_ready, t * U + (u + 2))
                                e.wait_ge(gsum_added, t * U + (u + 1))
                                to = gs[:, bass.ds(w_g[u], W)]
                                e.tensor_tensor(to, to, pM[:, 0:W], ALU.add).then_inc(gsum_added, 1)
                            ch.close()

        general_pass("sum")

        with ExitStack() as c2:
            rb = sb("rb", [P, GC], ctx=c2)
            mb = sb("mb", [P, 2, GC], ctx=c2)
            pL = ps("pL", [P, 2, 512], c2)
            r_in = sem("r_in")
            means_ready = sem("means_ready")
            deg_ready = sem("deg_ready")
            dg = sb("dg", [P, GC], ctx=c2)
            lin2_ready = sem("lin2_ready")
            group_done = sem("group_done")
            chain2 = sem("chain2")
            with nc.Block() as block:
                @block.sync
                def _(e):
                    with e.Fori(0, GROUPS) as t:
                        e.wait_ge(group_done, t + 1)
                        e.dma_start(rb[:, :], r_dram[:, bass.ds(t * GC, GC)]).then_inc(r_in, 16)

                @block.tensor
                def _(e):
                    with e.Fori(0, GROUPS) as t:
                        e.wait_ge(means_ready, t + 1)
                        for b in range(2):
                            ins = e.matmul(pL[:, b, 0:HALF], k("W_l"), mb[:, 1, b * HALF:(b + 1) * HALF],
                                           start=True, stop=True)
                        ins.then_inc(lin2_ready, 1)

                @block.scalar
                def _(e):
                    with e.Fori(0, GROUPS) as t:
                        e.wait_ge(group_done, t + 1)
                        e.activation(dg[:, :], ac[:, 1, bass.ds(t * GC, GC)], ACT.Sqrt,
                                     bias=k("ones")[:, 0:1]).then_inc(deg_ready, 1)

                @block.vector
                def _(e):
                    e.sem_inc(group_done, 1)
                    with e.Fori(0, GROUPS) as t:
                        ch = Chain(e, chain2, t, 5, passed)
                        cols = bass.ds(t * GC, GC)
                        ch.then(e.tensor_scalar(mb[:, 0, :], ac[:, 1, cols], 1.0, None, ALU.max))
                        ch.wait()
                        ch.then(e.reciprocal(mb[:, 1, :], mb[:, 0, :]))
                        ch.wait()
                        e.tensor_tensor(mb[:, 1, :], ac[:, 0, cols], mb[:, 1, :], ALU.mult).then_inc(means_ready, 1)
                        wait_alone(e, deg_ready, t + 1, passed)
                        ch.then(e.reciprocal(ac[:, 1, cols], dg[:, :]))
                        e.wait_ge(r_in, t * 16 + 16)
                        ch.then(e.tensor_tensor(gs[:, cols], gs[:, cols], rb[:, :], ALU.add))
                        ch.wait()
                        e.wait_ge(lin2_ready, t + 1)
                        to = gs[:, cols].rearrange("p (a b) -> p a b", a=2)
                        ch.then(e.tensor_tensor(to, to, pL[:, :, 0:HALF], ALU.add))
                        ch.wait()
                        e.sem_inc(group_done, 1)
                        ch.close()

        general_pass("gate")

        with ExitStack() as c2:
            bs = sb("bs", [P, N // BN_PIECE, 6], ctx=c2)
            bn_std = sem("bn_std")
            bn_chain = sem("bn_chain")
            with nc.Block() as block:
                @block.scalar
                def _(e):
                    e.wait_ge(bn_chain, 2)
                    e.activation(bn[:, 7:8], bn[:, 1:2], ACT.Sqrt, bias=k("eps")).then_inc(bn_std, 1)

                @block.vector
                def _(e):
                    for i in range(N // BN_PIECE):
                        ins = e.bn_stats(bs[:, i, :], gs[:, i * BN_PIECE:(i + 1) * BN_PIECE])
                    ins.then_inc(bn_chain, 1)
                    e.wait_ge(bn_chain, 1)
                    e.bn_aggr(bn[:, 0:2], bs[:, :, :]).then_inc(bn_chain, 1)
                    e.wait_ge(bn_std, 1)
                    e.reciprocal(bn[:, 2:3], bn[:, 7:8]).then_inc(bn_chain, 1)
                    e.wait_ge(bn_chain, 3)
                    e.scalar_tensor_tensor(out=bn[:, 3:4], in0=bn[:, 2:3], scalar=2.0, in1=k("gamma"),
                                           op0=ALU.mult, op1=ALU.mult).then_inc(bn_chain, 1)
                    e.tensor_scalar(bn[:, 4:5], k("beta"), 2.0, None, ALU.mult).then_inc(bn_chain, 1)
                    e.wait_ge(bn_chain, 5)
                    e.tensor_tensor(bn[:, 5:6], bn[:, 0:1], bn[:, 3:4], ALU.mult).then_inc(bn_chain, 1)
                    e.wait_ge(bn_chain, 6)
                    e.tensor_tensor(bn[:, 6:7], bn[:, 4:5], bn[:, 5:6], ALU.subtract).then_inc(bn_chain, 1)
                    e.wait_ge(bn_chain, 7)

        x2 = ac[:, 0, 0:NP].rearrange("p (t d) -> p t d", d=D)

        with ExitStack() as c3:
            xb = sb("x3", [P, GT, D], ctx=c3)
            yT = sb("y3", [P, GC], ctx=c3)
            hb = sb("h3", [P, GT, D], ctx=c3)
            hT = sb("hT3", [P, GC], ctx=c3)
            hsb = sb("hs3", [P, GT, HID], ctx=c3)
            st = sb("st3", [P, GT, 6], ctx=c3)
            mv = sb("mv3", [P, GT, 2], ctx=c3)
            rs = sb("rs3", [P, GT], ctx=c3)
            nb = sb("nb3", [P, GT], ctx=c3)
            dc = sb("dc3", [P, 8], ctx=c3)
            dT = sb("dT3", [P, GC], ctx=c3)
            pT = ps("pT3", [P, 1024], c3)
            pH = ps("pH3", [P, 512], c3)
            pS = ps("pS3", [HID, 2, 512], c3)
            pD = ps("pD3", [P, 8], c3)
            x3_in = sem("x3_in")
            y_ready = sem("y_ready")
            yT_ready = sem("yT_ready")
            x2_ready = sem("x2_ready")
            stats3_ready = sem("stats3_ready")
            var3_ready = sem("var3_ready")
            std3_ready = sem("std3_ready")
            sd = sb("sd3", [P, GT], ctx=c3)
            h3_ready = sem("h3_ready")
            hT3_ready = sem("hT3_ready")
            hT3_copied = sem("hT3_copied")
            conv_ready = sem("conv_ready")
            hs_ready = sem("hs_ready")
            hs_out = sem("hs_out")
            hs_free = sem("hs_free")
            chain3 = sem("chain3")
            with nc.Block() as block:
                @block.sync
                def _(e):
                    with e.Fori(0, GROUPS) as t:
                        e.wait_ge(hs_ready, t + 1)
                        e.dma_start(xb[:, :, :], xg[t]).then_inc(x3_in, 16)

                @block.gpsimd
                def _(e):
                    with e.Fori(0, GROUPS) as t:
                        e.wait_ge(hs_ready, t + 2)
                        e.dma_start(hsg[t], hsb[:, :, :]).then_inc(hs_out, 16)
                        e.wait_ge(hs_out, t * 16 + 16)
                        e.sem_inc(hs_free, 1)

                @block.scalar
                def _(e):
                    with e.Fori(0, GROUPS) as t:
                        e.wait_ge(hs_ready, t + 1)
                        e.activation(yT[:, :], gs[:, bass.ds(t * GC, GC)], ACT.Relu, bias=bn[:, 6:7],
                                     scale=bn[:, 3:4]).then_inc(y_ready, 1)
                        e.wait_ge(var3_ready, t + 1)
                        e.activation(sd[:, :], mv[:, :, 1], ACT.Sqrt, bias=k("eps")).then_inc(std3_ready, 1)
                        e.wait_ge(stats3_ready, t + 1)
                        for j in range(GT):
                            ins = e.activation(hb[:, j, :], x2[:, bass.ds(t * GT + j, 1), :]
                                               .rearrange("p o d -> p (o d)"), ACT.Relu,
                                               bias=nb[:, j:j + 1], scale=rs[:, j:j + 1])
                        ins.then_inc(h3_ready, 1)
                        e.wait_ge(hT3_ready, t + 1)
                        e.activation(hT[:, :], pT[:, 0:GC], ACT.Copy).then_inc(hT3_copied, 1)

                @block.tensor
                def _(e):
                    with e.Fori(0, GROUPS) as t:
                        e.wait_ge(y_ready, t + 1)
                        for j in range(GT):
                            ins = e.transpose(pT[:, j * P:(j + 1) * P], yT[:, j * P:(j + 1) * P], k("ident"))
                        ins.then_inc(yT_ready, 1)
                        e.wait_ge(h3_ready, t + 1)
                        for j in range(GT):
                            ins = e.transpose(pT[:, j * P:(j + 1) * P], hb[:, j, :], k("ident"))
                        ins.then_inc(hT3_ready, 1)
                        e.wait_ge(hT3_copied, t + 1)
                        for j in range(GT):
                            e.matmul(pD[:, j:j + 1], dT[:, j * P:(j + 1) * P], k("ident")[:, 0:1],
                                     start=True, stop=True)
                        for j in range(GT):
                            e.matmul(pH[:, j * HID:(j + 1) * HID], hT[:, j * P:(j + 1) * P], k("conv"),
                                     start=True, stop=True)
                        for b in range(2):
                            ins = e.matmul(pS[:, b, 0:HALF], k("conv"), hT[:, b * HALF:(b + 1) * HALF],
                                           start=True, stop=True)
                        ins.then_inc(conv_ready, 1)

                @block.vector
                def _(e):
                    e.sem_inc(hs_ready, 1)
                    e.sem_inc(hs_free, 1)
                    with e.Fori(0, GROUPS) as t:
                        ch = Chain(e, chain3, t, 6, passed)
                        cols = bass.ds(t * GC, GC)
                        x2g = x2[:, bass.ds(t * GT, GT), :]
                        e.wait_ge(x3_in, t * 16 + 16)
                        e.wait_ge(yT_ready, t + 1)
                        ch.then(e.tensor_tensor(x2g, xb[:, :, :],
                                                pT[:, 0:GC].rearrange("p (t d) -> p t d", d=D), ALU.add))
                        ch.then(e.tensor_copy(dT[:, :], ac[:, 1, cols]))
                        ch.wait()
                        for j in range(GT):
                            ins = e.bn_stats(st[:, j, :], x2[:, bass.ds(t * GT + j, 1), :]
                                             .rearrange("p o d -> p (o d)"))
                        ch.then(ins)
                        ch.wait()
                        for j in range(GT):
                            ins = e.bn_aggr(mv[:, j, :], st[:, j, :])
                        ch.then(ins)
                        ch.wait()
                        e.sem_inc(var3_ready, 1)
                        e.wait_ge(std3_ready, t + 1)
                        ch.then(e.reciprocal(rs[:, :], sd[:, :]))
                        ch.wait()
                        e.scalar_tensor_tensor(out=nb[:, :], in0=mv[:, :, 0], scalar=-1.0, in1=rs[:, :],
                                               op0=ALU.mult, op1=ALU.mult).then_inc(stats3_ready, 1)
                        e.wait_ge(conv_ready, t + 1)
                        e.tensor_tensor(gs[0:HID, cols].rearrange("p (a b) -> p a b", a=2), pS[:, :, 0:HALF],
                                        ac[0:HID, 1, cols].rearrange("p (a b) -> p a b", a=2), ALU.mult)
                        ch.then(e.tensor_copy(dc[:, 0:GT], pD[:, 0:GT]))
                        ch.wait()
                        e.wait_ge(hs_free, t + 1)
                        e.tensor_tensor(hsb[:, :, :], pH[:, 0:GT * HID].rearrange("p (t f) -> p t f", f=HID),
                                        dc[:, 0:GT].rearrange("p (t o) -> p t o", o=1)
                                        .to_broadcast((P, GT, HID)), ALU.mult).then_inc(hs_ready, 1)
                        ch.close()

        with ExitStack() as c4:
            g = sb("g4", [P, U, CT, HID], ctx=c4)
            ix = sb("ix4", [P, 2, 2 * CT], I32, ctx=c4)
            oh = sb("oh4", [P, 2, CT, W], ctx=c4)
            pA = ps("pA4", [HID, 2, 512], c4)
            ix_in = [sem("ix4_in0"), sem("ix4_in1")]
            g_in = [sem(f"g4_in{u}") for u in range(U)]
            oh_ready = sem("oh4_ready")
            sums_ready = sem("sums4_ready")
            sums_added = sem("sums4_added")
            TURNS = CHUNKS // U
            with nc.Block() as block:
                @block.sync
                def _(e):
                    with e.If(takes_fast_path(e)):
                        with e.Fori(0, TURNS) as t:
                            for h in range(2):
                                e.wait_ge(sums_ready, t * U + (2 * h + 2))
                                e.dma_start(ix[:, h, :], src[:, bass.ds(t * (U * CT) + 2 * h * CT, 2 * CT)])\
                                    .then_inc(ix_in[h], 16)

                @block.gpsimd
                def _(e):
                    with e.If(takes_fast_path(e)):
                        with e.Fori(0, TURNS) as t:
                            for u in range(U):
                                if u % 2 == 0:
                                    wait_alone(e, ix_in[u // 2], t * 16 + 16, passed)
                                wait_alone(e, sums_ready, t * U + (u + 1), passed)
                                for j in range(CT):
                                    c = (u % 2) * CT + j
                                    e.indirect_dma_start(
                                        g[:, u, j, :], None, hs_dram,
                                        bass.IndirectOffsetOnAxis(ap=ix[:, u // 2, c:c + 1], axis=0)
                                    ).then_inc(g_in[u], 16)

                @block.tensor
                def _(e):
                    with e.If(takes_fast_path(e)):
                        e.sem_inc(sums_ready, U)
                        with e.Fori(0, TURNS) as t:
                            for u in range(U):
                                e.wait_ge(oh_ready, t * U + (u + 1))
                                e.wait_ge(sums_added, t * U + (u + 1))
                                e.wait_ge(g_in[u], t * (16 * CT) + 16 * CT)
                                for j in range(CT):
                                    ins = e.matmul(pA[:, u % 2, 0:W], g[:, u, j, :], oh[:, u % 2, j, :],
                                                   start=(j == 0), stop=(j == CT - 1))
                                ins.then_inc(sums_ready, 1)

                @block.vector
                def _(e):
                    with e.If(takes_fast_path(e)):
                        e.sem_inc(sums_added, 2)

                        def one_hot(to, s):
                            return e.tensor_tensor(
                                to, relf[:, bass.ds(s, 1), :].rearrange("p s (c o) -> p (s c) o", o=1)
                                .to_broadcast((P, CT, W)),
                                k("iota").rearrange("p (o w) -> p o w", o=1).to_broadcast((P, CT, W)),
                                ALU.is_equal)

                        one_hot(oh[:, 0, :, :], FRONT).then_inc(oh_ready, 1)
                        with e.Fori(0, TURNS) as t:
                            for u in range(U):
                                e.wait_ge(sums_ready, t * U + (u + U))
                                one_hot(oh[:, 1 - u % 2, :, :], t * U + (u + FRONT + 1)).then_inc(oh_ready, 1)
                                wk = e.value_load(base_i[0:1, bass.ds(t * U + (u + FRONT), 1)],
                                                  min_val=0, max_val=NW - W)
                                e.wait_ge(sums_ready, t * U + (u + U + 1))
                                e.wait_ge(sums_added, t * U + (u + 2))
                                to = gs[0:HID, bass.ds(wk, W)]
                                e.tensor_tensor(to, to, pA[:, u % 2, 0:W], ALU.add).then_inc(sums_added, 1)

        general_pass("conv")

        with ExitStack() as c5:
            z = sb("z", [P, 2, GC], ctx=c5)
            ob = sb("ob", [P, 2, GT, D], ctx=c5)
            pZ = ps("pZ", [P, 2, 1024], c5)
            z0_ready = sem("z0_ready")
            z_ready = sem("z_ready")
            y2_ready = sem("y2_ready")
            o_ready = sem("o_ready")
            o_out = [sem("o_out0"), sem("o_out1")]
            o_free = sem("o_free")
            z_one = sem("z_one")
            zf = sb("zf", [HID, 2, GC], ctx=c5)
            with nc.Block() as block:
                @block.sync
                def _(e):
                    e.sem_inc(o_free, 2)
                    with e.Fori(0, GROUPS // 2) as t:
                        for u in range(2):
                            e.wait_ge(o_ready, t * 2 + (u + 1))
                            e.dma_start(og[t * 2 + u], ob[:, u, :, :]).then_inc(o_out[u], 16)
                        for u in range(2):
                            e.wait_ge(o_out[u], t * 16 + 16)
                            e.sem_inc(o_free, 1)
                    e.wait_ge(o_out[0], 16 * (GROUPS // 2))
                    e.wait_ge(o_out[1], 16 * (GROUPS // 2))

                @block.vector
                def _(e):
                    e.memset(z[HID:HID + 32, :, :], 1.0).then_inc(z_one, 1)
                    e.wait_ge(z_one, 1)
                    e.sem_inc(z_ready, 2)
                    with e.Fori(0, GROUPS // 2) as t:
                        for u in range(2):
                            cols = bass.ds((t * 2 + u) * GC, GC)
                            e.wait_ge(z_ready, t * 2 + (u + 1))
                            e.tensor_tensor(zf[:, u, :], gs[0:HID, cols], ac[0:HID, 1, cols], ALU.mult)\
                                .then_inc(z0_ready, 1)
                            e.wait_ge(y2_ready, t * 2 + (u + 1))
                            e.wait_ge(o_free, t * 2 + (u + 1))
                            e.tensor_tensor(ob[:, u, :, :], x2[:, bass.ds((t * 2 + u) * GT, GT), :],
                                            pZ[:, u, 0:GC].rearrange("p (t d) -> p t d", d=D), ALU.add)\
                                .then_inc(o_ready, 1)

                @block.scalar
                def _(e):
                    with e.Fori(0, GROUPS // 2) as t:
                        for u in range(2):
                            e.wait_ge(z0_ready, t * 2 + (u + 1))
                            e.activation(z[0:HID, u, :], zf[:, u, :], ACT.Relu, bias=k("b_conv", HID))\
                                .then_inc(z_ready, 1)

                @block.tensor
                def _(e):
                    e.wait_ge(z_one, 1)
                    with e.Fori(0, GROUPS // 2) as t:
                        for u in range(2):
                            e.wait_ge(z_ready, t * 2 + (u + 3))
                            for j in range(GT):
                                ins = e.matmul(pZ[:, u, j * P:(j + 1) * P], z[0:HID + 1, u, j * P:(j + 1) * P],
                                               k("lin", HID + 1), start=True, stop=True)
                            ins.then_inc(y2_ready, 1)


def kernel(x, src, dst, edge_attr_32, L0_gnn_W_emb, L0_gnn_b_emb, L0_gnn_W_temb, L0_gnn_b_temb,
           L0_gnn_W_tattr, L0_gnn_b_tattr, L0_gnn_W_gate, L0_gnn_b_gate, L0_gnn_W_l, L0_gnn_b_l,
           L0_gnn_W_r, L0_gnn_gamma, L0_gnn_beta, L1_gnn_W_conv, L1_gnn_b_conv, L1_gnn_W_lin,
           L1_gnn_b_lin):
    from concourse import bacc
    from concourse.bass_utils import run_bass_kernel_spmd

    f = np.float32
    x = np.asarray(x)
    src_k = np.zeros(((STEPS + U) * EC,), np.int32)
    src_k[0:E] = src
    dst_k = np.full((SLOTS * EC,), N, np.int32)
    dst_k[FRONT * EC:FRONT * EC + E] = dst
    ea_k = np.zeros((SLOTS * EC, EA), f)
    ea_k[FRONT * EC:FRONT * EC + E] = edge_attr_32

    keep = np.zeros((P, KEEP_N), f)
    once = np.zeros((P, ONCE_N), f)

    def put(to, at, name, a, row=0, col=0):
        lo = at[name][0] + col
        a = np.asarray(a)
        to[row:row + a.shape[0], lo:lo + a.shape[1]] = a

    def keeps(*a, **kw):
        put(keep, KEEP_AT, *a, **kw)

    def onces(*a, **kw):
        put(once, ONCE_AT, *a, **kw)

    W_g = np.asarray(L0_gnn_W_gate)
    keeps("W_l", L0_gnn_W_l)
    keeps("W_g1", W_g[0:D])
    keeps("ident", np.eye(P, dtype=f))
    keeps("ones", np.ones((P, P), f))
    keeps("lin", L1_gnn_W_lin)
    keeps("lin", np.asarray(L1_gnn_b_lin)[None, :], row=HID)
    keeps("conv", L1_gnn_W_conv)
    keeps("iota", np.tile(np.arange(W, dtype=f), (P, 1)))
    keeps("b_l", np.asarray(L0_gnn_b_l)[:, None])
    keeps("gamma", np.asarray(L0_gnn_gamma)[:, None])
    keeps("beta", np.asarray(L0_gnn_beta)[:, None])
    keeps("b_conv", np.asarray(L1_gnn_b_conv)[:, None])
    keeps("pmod", (np.arange(P) % W).astype(f)[:, None])
    keeps("spare", (NP + np.arange(P)).astype(f)[:, None])
    keeps("before", np.tri(P, k=-1, dtype=f))
    keeps("eps", np.full((P, 1), EPS, f))
    for c in range(U):
        keeps("emb", L0_gnn_W_emb, row=EA * c, col=EA * c)
        keeps("b_emb", np.asarray(L0_gnn_b_emb)[:, None], row=EA * c)
    onces("AT", np.asarray(L0_gnn_W_tattr).T)
    onces("AT", np.asarray(L0_gnn_W_temb).T, col=EA)
    onces("AT", np.asarray(L0_gnn_b_temb)[:, None], col=ONE)
    onces("BT", np.asarray(L0_gnn_W_tattr).T)
    onces("BT", np.asarray(L0_gnn_b_tattr)[:, None], col=ONE)
    onces("CT", np.asarray(L0_gnn_b_tattr)[:, None], col=ONE)
    onces("e_one", np.ones((1, 1), f), col=ONE)
    onces("W_g2", W_g[D:2 * D])
    onces("W_g3", W_g[2 * D:3 * D])
    onces("W_r", L0_gnn_W_r)
    onces("W_lT", np.asarray(L0_gnn_W_l).T)
    onces("b_gate", np.asarray(L0_gnn_b_gate)[None, :])

    x_p = np.zeros((NP, D), f)
    x_p[0:N] = x
    arrays = {
        "x": x_p,
        "src": np.ascontiguousarray(src_k.reshape(STEPS + U, CT, P).transpose(2, 0, 1).reshape(P, -1)),
        "dst": np.ascontiguousarray(dst_k.reshape(SLOTS, CT, P).transpose(2, 0, 1)),
        "dst_row": dst_k.reshape(1, SLOTS, EC),
        "base": np.ascontiguousarray(dst_k[::EC][None, :]),
        "last": np.ascontiguousarray(dst_k[EC - 1::EC][None, :]),
        "ea": np.ascontiguousarray(ea_k.T).reshape(EA, SLOTS, EC),
        "ea4": np.ascontiguousarray(
            ea_k[(FRONT + 1 - LAG) * EC:(FRONT + 1 - LAG + STEPS + U) * EC].reshape(-1, U, EC, EA)
            .transpose(1, 3, 0, 2).reshape(P, -1, EC)),
        "keep": keep,
        "once": once,
    }
    nc = bacc.Bacc("TRN2", target_bir_lowering=False, num_devices=1)
    args = {n: nc.dram_tensor(n, a.shape, mybir.dt.from_np(a.dtype), kind="ExternalInput").ap()
            for n, a in arrays.items()}
    args["out"] = nc.dram_tensor("out", (NP, D), F32, kind="ExternalOutput").ap()
    gnn_two_layers(nc, **args)
    r = run_bass_kernel_spmd(nc, [arrays], core_ids=[0])
    return r.results[0]["out"][0:N]
```

```python
from contextlib import ExitStack

import numpy as np

import concourse.bass as bass
from concourse import mybir

F32 = mybir.dt.float32
I32 = mybir.dt.int32
BF16 = mybir.dt.bfloat16
ALU = mybir.AluOpType
ACT = mybir.ActivationFunctionType
AX = mybir.AxisListType

P = 128
N = 12500
E = 400000
D = 128
HID = 64
EA, EE = 32, 16
ONE = EA + EE
EPS = 1e-5

W = 64
CT = 4
EC = CT * P
U = 4
CHUNKS = -(-E // (EC * U)) * U
LAG = 13
REACH = LAG - 1
DRAIN = -(-(LAG + 1) // U) * U
STEPS = CHUNKS + DRAIN
FRONT = DRAIN
SLOTS = FRONT + STEPS + U

NT = -(-N // P)
NP = NT * P
NW = NP + W
GT = 7
GC = GT * P
GROUPS = NT // GT
HALF = GC // 2
BN_PIECE = 500

KEEP = ["W_l", "W_g1", "emb", "ident", "ones", "lin", "conv", "iota", "b_l", "gamma", "beta",
        "b_conv", "pmod", "eps", "b_emb", "spare", "before"]
KEEP_W = [D, D, D, P, P, D, HID, W, 1, 1, 1, 1, 1, 1, 1, 1, P]
ONCE = ["AT", "BT", "CT", "W_g2", "W_g3", "W_r", "e_one", "b_gate", "W_lT"]
ONCE_W = [P, P, P, D, D, D, P, D, P]


def columns(names, widths):
    at, out = 0, {}
    for n, w in zip(names, widths):
        out[n] = (at, at + w)
        at += w
    return out, at


KEEP_AT, KEEP_N = columns(KEEP, KEEP_W)
ONCE_AT, ONCE_N = columns(ONCE, ONCE_W)
assert GROUPS * GT == NT and CHUNKS % U == 0 and STEPS % U == 0 and N % BN_PIECE == 0


def wait_alone(eng, sem, value, passed):
    eng.wait_ge(sem, value)
    eng.sem_inc(passed, 1)


class Chain:

    def __init__(self, eng, sem, turn, per_turn, passed):
        self.eng, self.sem, self.turn, self.per_turn, self.n = eng, sem, turn, per_turn, 0
        self.passed = passed

    def then(self, ins):
        self.n += 1
        ins.then_inc(self.sem, 1)

    def wait(self):
        wait_alone(self.eng, self.sem, self.turn * self.per_turn + self.n, self.passed)

    def close(self):
        assert self.n == self.per_turn, self.n


def gnn_two_layers(nc, x, src, dst, dst_row, base, last, ea, ea4, keep, once, out):
    rg_dram = nc.dram_tensor("rg_dram", (NW, D), F32).ap()
    h_dram = nc.dram_tensor("h_dram", (NP, 3 * D), BF16).ap()
    hs_dram = nc.dram_tensor("hs_dram", (NP, HID), F32).ap()
    xg = x.rearrange("(g j p) d -> g p j d", j=GT, p=P)
    hg = h_dram.rearrange("(g j p) d -> g p j d", j=GT, p=P)
    hsg = hs_dram.rearrange("(g j p) d -> g p j d", j=GT, p=P)
    rgg = rg_dram[0:NP, :].rearrange("(g j p) d -> g p j d", j=GT, p=P)
    count_dram = nc.dram_tensor("count_dram", (NT, P), F32).ap()
    share_dram = nc.dram_tensor("share_dram", (NT, P), F32).ap()
    norm_dram = nc.dram_tensor("norm_dram", (NT, P), F32).ap()
    og = out.rearrange("(g j p) d -> g p j d", j=GT, p=P)

    RUN = CHUNKS * EC // P
    dst_cols = dst.rearrange("p s c -> p (s c)")
    ea_cols = ea.rearrange("f s c -> f (s c)")
    rows = dst_row.rearrange("o s c -> o (s c)")

    with ExitStack() as kept:
        def sb(name, shape, dt=F32, ctx=kept):
            return ctx.enter_context(nc.sbuf_tensor(name, shape, dt))

        def ps(name, shape, ctx):
            return ctx.enter_context(nc.psum_tensor(name, shape, F32))

        def sem(name):
            return kept.enter_context(nc.semaphore(name))

        passed = sem("passed")

        ac = sb("ac", [P, 2, NW])
        gs = sb("gs", [P, NW])
        rel = sb("rel", [P, SLOTS, CT], I32)
        relf = rel[:, :, :].bitcast(F32)
        base_p = sb("base_p", [P, SLOTS])
        base_i = sb("base_i", [1, SLOTS], I32)
        kp = sb("kp", [P, KEEP_N])
        wt = sb("wt", [P, 2 * D])
        wlg = sb("wlg", [P, D])

        def k(name, rows=P):
            a, b = KEEP_AT[name]
            return kp[0:rows, a:b]

        flag = sb("flag", [1, 4], I32)
        norm = sb("norm", [P, NT])
        bn = sb("bn", [P, 8])

        def takes_fast_path(e):
            return e.value_load(flag[0:1, 0:1], min_val=0, max_val=4 * P) == 0

        def general_pass(kind):
            DW = {"sum": 2 * D, "gate": D, "conv": HID}[kind]
            rows_of = {"sum": (h_dram, 3 * D, BF16), "gate": (None, D, F32), "conv": (hs_dram, HID, F32)}[kind]
            acc = nc.dram_tensor(f"acc_{kind}", (NP + P, DW), F32).ap()
            ow_dram = nc.dram_tensor(f"ow_{kind}", (NP, D), F32).ap() if kind == "gate" else None
            table = ow_dram if kind == "gate" else rows_of[0]
            TILES = CHUNKS * CT
            with ExitStack() as c:
                def sbk(name, shape, dt=F32):
                    return sb(f"{name}_{kind}", shape, dt, ctx=c)

                def semk(name):
                    return sem(f"{name}_{kind}")

                got = sbk("got", [P, rows_of[1]], rows_of[2])
                ic = sbk("ic", [P, 1], I32)
                dc = sbk("dc", [P, 1], I32)
                dr = sbk("dr", [P, P], I32)
                dcf = sbk("dcf", [P, 1])
                eq = sbk("eq", [P, P])
                ev = sbk("ev", [P, P])
                ne = sbk("ne", [P, 4])
                to = sbk("to", [P, 1], I32)
                va = sbk("va", [P, DW])
                vs = sbk("vs", [P, DW])
                ft = sbk("ft", [P, P])
                gate = sbk("gate", [P, D])
                pS = ps(f"pS_{kind}", [P, 512], c)
                pF = ps(f"pF_{kind}", [P, 512], c)
                pE = ps(f"pE_{kind}", [P, 512], c)
                zeros_ready, zeros_out = semk("zeros_ready"), semk("zeros_out")
                if kind == "gate":
                    blk_in, blk_ready, blk_out, blk_copied = (semk("blk_in"), semk("blk_ready"),
                                                              semk("blk_out"), semk("blk_copied"))
                    emb_in, emb_ready, feat_ready, pre_ready, gate_ready = (
                        semk("emb_in"), semk("emb_ready"), semk("feat_ready"), semk("pre_ready"),
                        semk("gate_ready"))
                tile_in, got_in, added, tile_free = (semk("tile_in"), semk("got_in"), semk("added"),
                                                     semk("tile_free"))
                to_ready, va_ready, sum_ready, vs_ready = (semk("to_ready"), semk("va_ready"),
                                                           semk("sum_ready"), semk("vs_ready"))
                acc_in, turned, merged = semk("acc_in"), semk("turned"), semk("merged")
                chain = semk("chain")
                LOADS = 4 if kind == "gate" else 3
                with nc.Block() as block:
                    @block.sync
                    def _(e):
                        with e.If(takes_fast_path(e)):
                            pass
                        with e.Else():
                            e.wait_ge(zeros_ready, 1)
                            with e.Fori(0, NT + 1) as t:
                                e.dma_start(acc[bass.ds(t * P, P), :], va[:, :]).then_inc(zeros_out, 16)
                            e.wait_ge(zeros_out, 16 * (NT + 1))
                            e.sem_inc(tile_free, 1)
                            if kind == "gate":
                                with e.Fori(0, NT) as t:
                                    wait_alone(e, blk_copied, t + 1, passed)
                                    e.dma_start(ow_dram[bass.ds(t * P, P), :], gate[:, :]).then_inc(blk_out, 16)
                                    e.wait_ge(blk_out, t * 16 + 16)
                                    e.sem_inc(blk_in, 1)
                            with e.Fori(0, TILES) as t:
                                wait_alone(e, tile_free, t + 1, passed)
                                if kind == "gate":
                                    e.dma_start(ic[:, :], dst_cols[:, bass.ds(t + FRONT * CT, 1)],
                                                allow_slow_non_contiguous=True)\
                                        .then_inc(tile_in, 16)
                                    e.dma_start(ft[0:EA, :], ea_cols[:, bass.ds(t * P + FRONT * EC, P)])\
                                        .then_inc(tile_in, 16)
                                else:
                                    e.dma_start(ic[:, :], src[:, bass.ds(t, 1)], allow_slow_non_contiguous=True).then_inc(tile_in, 16)
                                e.dma_start(dc[:, :], dst_cols[:, bass.ds(t + FRONT * CT, 1)],
                                            allow_slow_non_contiguous=True).then_inc(tile_in, 16)
                                e.dma_start(dr[:, :], rows[:, bass.ds(t * P + FRONT * EC, P)]
                                            .to_broadcast((P, P))).then_inc(tile_in, 16)
                            e.wait_ge(tile_free, TILES + 1)
                            with e.Fori(0, NT) as t:
                                wait_alone(e, merged, t + 1, passed)
                                e.dma_start(vs[:, :], acc[bass.ds(t * P, P), :]).then_inc(acc_in, 16)

                    @block.gpsimd
                    def _(e):
                        with e.If(takes_fast_path(e)):
                            pass
                        with e.Else():
                            if kind == "gate":
                                e.wait_ge(blk_in, NT + 1)
                            with e.Fori(0, TILES) as t:
                                wait_alone(e, tile_in, t * (16 * LOADS) + 16 * LOADS, passed)
                                e.indirect_dma_start(got[:, :], None, table,
                                                     bass.IndirectOffsetOnAxis(ap=ic[:, 0:1], axis=0))\
                                    .then_inc(got_in, 16)
                                wait_alone(e, to_ready, t + 1, passed)
                                wait_alone(e, vs_ready, t + 1, passed)
                                e.indirect_dma_start(acc, bass.IndirectOffsetOnAxis(ap=to[:, 0:1], axis=0),
                                                     vs[:, :], None, compute_op=ALU.add).then_inc(added, 16)
                                e.wait_ge(added, t * 16 + 16)
                                e.sem_inc(tile_free, 1)

                    @block.tensor
                    def _(e):
                        with e.If(takes_fast_path(e)):
                            pass
                        with e.Else():
                            if kind == "gate":
                                with e.Fori(0, NT) as t:
                                    e.wait_ge(blk_ready, t + 1)
                                    e.matmul(pS[:, 0:D], eq[:, :], k("W_g1"), start=True, stop=True)\
                                        .then_inc(turned, 1)
                            with e.Fori(0, TILES) as t:
                                if kind == "gate":
                                    wait_alone(e, tile_in, t * (16 * LOADS) + 16 * LOADS, passed)
                                    e.matmul(pE[0:EE, 0:P], k("emb")[0:EA, 0:EE], ft[0:EA, :],
                                             start=True, stop=True).then_inc(emb_in, 1)
                                    e.wait_ge(emb_ready, t + 1)
                                    e.matmul(pF[:, 0:2 * D], ft[0:64, :], wt[0:64, :], start=True, stop=True)\
                                        .then_inc(feat_ready, 1)
                                e.wait_ge(to_ready, t + 1)
                                e.wait_ge(va_ready, t + 1)
                                e.matmul(pS[:, 0:DW], eq[:, :], va[:, :], start=True, stop=True)\
                                    .then_inc(sum_ready, 1)
                            with e.Fori(0, NT) as t:
                                wait_alone(e, acc_in, t * 16 + 16, passed)
                                for b in range(2 if kind == "sum" else 1):
                                    ins = e.transpose(pS[0:min(DW, P), b * P:(b + 1) * P],
                                                      vs[:, b * P:min(DW, (b + 1) * P)], k("ident"))
                                ins.then_inc(turned, 1)

                    @block.scalar
                    def _(e):
                        with e.If(takes_fast_path(e)):
                            pass
                        with e.Else():
                            if kind == "gate":
                                e.wait_ge(zeros_ready, 1)
                                with e.Fori(0, TILES) as t:
                                    e.wait_ge(emb_in, t + 1)
                                    e.activation(ft[EA:ONE, :], pE[0:EE, 0:P], ACT.Relu,
                                                 bias=k("b_emb")[0:EE, :]).then_inc(emb_ready, 1)
                                    e.wait_ge(pre_ready, t + 1)
                                    e.activation(gate[:, :], gate[:, :], ACT.Sigmoid).then_inc(gate_ready, 1)

                    @block.vector
                    def _(e):
                        with e.If(takes_fast_path(e)):
                            pass
                        with e.Else():
                            e.memset(ft[:, :], 1.0)
                            e.memset(va[:, :], 0.0).then_inc(zeros_ready, 1)
                            e.sem_inc(merged, 1)
                            e.wait_ge(zeros_out, 16 * (NT + 1))
                            if kind == "sum":
                                e.memset(va[:, :], 1.0)
                            if kind == "gate":
                                e.sem_inc(blk_in, 1)
                                with e.Fori(0, NT) as t:
                                    e.wait_ge(blk_in, t + 1)
                                    e.tensor_copy(eq[:, :], gs[:, bass.ds(t * P, P)]).then_inc(blk_ready, 1)
                                    e.wait_ge(turned, t + 1)
                                    e.tensor_copy(gate[:, :], pS[:, 0:D]).then_inc(blk_copied, 1)
                            PER = {"sum": 7, "gate": 6, "conv": 6}[kind]
                            with e.Fori(0, TILES) as t:
                                ch = Chain(e, chain, t, PER, passed)
                                wait_alone(e, tile_in, t * (16 * LOADS) + 16 * LOADS, passed)
                                ch.then(e.tensor_copy(dcf[:, :], dc[:, :]))
                                ch.wait()
                                ch.then(e.tensor_scalar(eq[:, :], dr[:, :], dcf[:, 0:1], None, ALU.is_equal))
                                ch.wait()
                                ch.then(e.tensor_tensor(ev[:, :], eq[:, :], k("before"), ALU.mult))
                                ch.wait()
                                ch.then(e.tensor_reduce(ne[:, 0:1], ev[:, :], AX.X, ALU.max))
                                ch.then(e.tensor_tensor(ne[:, 1:2], k("spare"), dcf[:, :], ALU.subtract))
                                ch.wait()
                                ch.then(e.tensor_tensor(ne[:, 2:3], ne[:, 1:2], ne[:, 0:1], ALU.mult))
                                ch.wait()
                                e.tensor_tensor(to[:, :], ne[:, 2:3], dcf[:, :], ALU.add).then_inc(to_ready, 1)
                                e.wait_ge(got_in, t * 16 + 16)
                                if kind == "sum":
                                    ch.then(e.tensor_tensor(ev[:, :], got[:, D:2 * D], got[:, 2 * D:3 * D], ALU.add))
                                    ch.wait()
                                    e.tensor_tensor(va[:, 0:D], ev[:, :], got[:, 0:D], ALU.add)\
                                        .then_inc(va_ready, 1)
                                elif kind == "gate":
                                    e.wait_ge(feat_ready, t + 1)
                                    e.tensor_tensor(gate[:, :], got[:, :], pF[:, 0:D], ALU.add)\
                                        .then_inc(pre_ready, 1)
                                    e.wait_ge(gate_ready, t + 1)
                                    e.tensor_tensor(va[:, :], gate[:, :], pF[:, D:2 * D], ALU.mult)\
                                        .then_inc(va_ready, 1)
                                else:
                                    e.tensor_copy(va[:, :], got[:, :]).then_inc(va_ready, 1)
                                e.wait_ge(sum_ready, t + 1)
                                e.tensor_copy(vs[:, :], pS[:, 0:DW]).then_inc(vs_ready, 1)
                                ch.close()
                            e.wait_ge(tile_free, TILES + 1)
                            with e.Fori(0, NT) as t:
                                e.wait_ge(turned, t + (NT + 1 if kind == "gate" else 1))
                                cols = bass.ds(t * P, P)
                                if kind == "sum":
                                    e.tensor_copy(ac[:, :, cols], pS[:, 0:2 * P]
                                                  .rearrange("p (a c) -> p a c", a=2)).then_inc(merged, 1)
                                else:
                                    e.tensor_tensor(gs[0:DW, cols], gs[0:DW, cols], pS[0:DW, 0:P], ALU.add)\
                                        .then_inc(merged, 1)

        with ExitStack() as c0:
            xb = sb("x0", [P, 2, GT, D], ctx=c0)
            hb = sb("h0", [P, GT, D], ctx=c0)
            hr = sb("hr0", [P, GT, D], ctx=c0)
            hp = sb("hp0", [P, 2, GT, 3 * D], BF16, ctx=c0)
            hT = sb("hT0", [P, GC], ctx=c0)
            rT = sb("rT0", [P, GC], ctx=c0)
            st = sb("st0", [P, GT, 6], ctx=c0)
            mv = sb("mv0", [P, GT, 2], ctx=c0)
            rs = sb("rs0", [P, GT], ctx=c0)
            nb = sb("nb0", [P, GT], ctx=c0)
            sd = sb("sd0", [P, GT], ctx=c0)
            temp = ac[:, 0, :]
            on = temp[:, 0:ONCE_N]
            at = ONCE_N
            baseb = temp[:, at:at + SLOTS].bitcast(I32)
            lastb = temp[:, at + SLOTS:at + 2 * SLOTS].bitcast(I32)
            at += 2 * SLOTS
            cur = temp[:, at:at + RUN]
            nxt = temp[:, at + RUN:at + 2 * RUN]
            at += 2 * RUN
            rgb = temp[:, at:at + GC].rearrange("p (t d) -> p t d", d=D)
            span = temp[:, at + GC:at + GC + CHUNKS]
            assert at + GC + CHUNKS <= NW
            vm = sb("vm", [P, 3], ctx=c0)
            vf = sb("vf", [P, 3], ctx=c0)
            fl = sb("fl", [1, 1], ctx=c0)
            pV = ps("pV", [P, 512], c0)
            viol_ready = sem("viol_ready")
            viol_sum = sem("viol_sum")
            flags = sem("flags")
            pT = ps("pT0", [P, 1024], c0)
            pR = ps("pR0", [P, 1024], c0)
            pW = ps("pW0", [P, 512], c0)
            pN = ps("pN0", [P, 1024], c0)

            def o(name, rows=P):
                a, b = ONCE_AT[name]
                return on[0:rows, a:b]

            consts_in = sem("consts_in")
            tables_in = sem("tables_in")
            x_in = [sem("x_in0"), sem("x_in1")]
            rows_out = [sem("rows_out0"), sem("rows_out1")]
            stored = sem("stored")
            r_kept = sem("r_kept")
            stats_ready, std_ready, scale_ready = sem("stats_ready"), sem("std_ready"), sem("scale_ready")
            h_ready, hi_ready, rest_ready, mid_ready, lo_ready = (
                sem("h_ready"), sem("hi_ready"), sem("rest_ready"), sem("mid_ready"), sem("lo_ready"))
            hT_ready, hT_copied, r_ready, rT_ready, rg_ready, rg_copied = (
                sem("hT_ready"), sem("hT_copied"), sem("r_ready"), sem("rT_ready"), sem("rg_ready"),
                sem("rg_copied"))
            pad_out = sem("pad_out")
            chain0 = sem("chain0")
            wt_ready = sem("wt_ready")
            zeroed = sem("zeroed")
            setup = sem("setup")
            T0 = GROUPS // 2

            def over_groups(e, head, tail):
                head(0, 0)
                with e.Fori(0, T0 - 1) as t:
                    for u in range(2):
                        head(t + u, 1 - u)
                        tail(t, u)
                head(T0 - 1, 1)
                tail(T0 - 1, 0)
                tail(T0 - 1, 1)

            with nc.Block() as block:
                @block.sync
                def _(e):
                    def load_x(t, u):
                        e.wait_ge(h_ready, t * 2 + (u + 1))
                        e.dma_start(xb[:, u, :, :], xg[t * 2 + u]).then_inc(x_in[u], 16)

                    def store(t, u):
                        e.wait_ge(lo_ready, t * 2 + (u + 2))
                        e.dma_start(hg[t * 2 + u], hp[:, u, :, :]).then_inc(rows_out[u], 16)
                        e.wait_ge(rg_copied, t * 2 + (u + 2))
                        e.dma_start(rgg[t * 2 + u], rgb[:, :, :]).then_inc(rows_out[u], 16)

                    load_x(0, 0)
                    load_x(0, 1)
                    e.dma_start(kp[:, :], keep).then_inc(consts_in, 16)
                    e.dma_start(on, once).then_inc(consts_in, 16)
                    e.dma_start(rel[:, :, :], dst).then_inc(tables_in, 16)
                    e.dma_start(base_i[:, :], base).then_inc(tables_in, 16)
                    e.dma_start(baseb, base.to_broadcast((P, SLOTS))).then_inc(tables_in, 16)
                    e.dma_start(lastb, last.to_broadcast((P, SLOTS))).then_inc(tables_in, 16)
                    for to, first in ((cur, FRONT * EC), (nxt, FRONT * EC + 1)):
                        e.dma_start(to.bitcast(I32), rows[:, first:first + P * RUN]
                                    .rearrange("o (p c) -> (o p) c", p=P)).then_inc(tables_in, 16)
                    with e.Fori(0, T0 - 1) as t:
                        for u in range(2):
                            load_x(t + 1, u)
                            store(t, u)
                    store(T0 - 1, 0)
                    store(T0 - 1, 1)

                @block.gpsimd
                def _(e):
                    def rest(t, u):
                        e.wait_ge(hi_ready, t * 2 + (u + 1))
                        e.wait_ge(lo_ready, t * 2 + (u + 1))
                        e.tensor_tensor(hr[:, :, :], hb[:, :, :], hp[:, u, :, 0:D], ALU.subtract)\
                            .then_inc(rest_ready, 1)

                    def landed(t, u):
                        wait_alone(e, rows_out[u], t * 32 + 32, passed)
                        e.sem_inc(stored, 1)

                    e.sem_inc(stored, 2)
                    e.memset(gs[:, NP:NW], 0.0).then_inc(zeroed, 1)
                    e.memset(ac[:, 1, :], 0.0).then_inc(zeroed, 1)
                    e.wait_ge(zeroed, 2)
                    e.dma_start(rg_dram[NP:NW, :], ac[0:W, 1, 0:D]).then_inc(pad_out, 16)
                    e.wait_ge(pad_out, 16)
                    over_groups(e, rest, landed)
                    e.wait_ge(flags, 6)
                    e.wait_ge(stored, GROUPS + 2)
                    e.memset(temp[:, NW // 2:NW], 0.0).then_inc(zeroed, 1)
                    e.wait_ge(zeroed, 3)

                @block.vector
                def _(e):
                    def head(t, u):
                        ch = Chain(e, chain0, t * 2 + u, 3, passed)
                        wait_alone(e, x_in[u], t * 16 + 16, passed)
                        for j in range(GT):
                            ins = e.bn_stats(st[:, j, :], xb[:, u, j, :])
                        ch.then(ins)
                        ch.wait()
                        for j in range(GT):
                            ins = e.bn_aggr(mv[:, j, :], st[:, j, :])
                        ch.then(ins)
                        ch.wait()
                        e.sem_inc(stats_ready, 1)
                        e.wait_ge(std_ready, t * 2 + (u + 1))
                        e.wait_ge(h_ready, t * 2 + (u + 2))
                        ch.then(e.reciprocal(rs[:, :], sd[:, :]))
                        ch.wait()
                        e.scalar_tensor_tensor(out=nb[:, :], in0=mv[:, :, 0], scalar=-1.0,
                                               in1=rs[:, :], op0=ALU.mult, op1=ALU.mult)\
                            .then_inc(scale_ready, 1)
                        ch.close()

                    def tail(t, u):
                        e.wait_ge(hT_ready, t * 2 + (u + 2))
                        e.wait_ge(r_ready, t * 2 + (u + 1))
                        e.tensor_copy(hT[:, :], pT[:, 0:GC]).then_inc(hT_copied, 1)
                        e.wait_ge(mid_ready, t * 2 + (u + 1))
                        e.tensor_tensor(hp[:, u, :, 2 * D:3 * D], hr[:, :, :], hp[:, u, :, D:2 * D],
                                        ALU.subtract).then_inc(lo_ready, 1)
                        e.wait_ge(r_ready, t * 2 + (u + 2))
                        e.wait_ge(rg_ready, t * 2 + (u + 1))
                        r = pR[:, :].rearrange("p (a b) -> p a b", a=2)[:, :, 0:HALF]
                        e.tensor_scalar(rT[:, :].rearrange("p (a b) -> p a b", a=2), r, k("b_l"), None,
                                        ALU.add).then_inc(rT_ready, 1)
                        e.tensor_scalar(gs[:, bass.ds((t * 2 + u) * GC, GC)].rearrange("p (a b) -> p a b", a=2),
                                        r, k("b_l"), None, ALU.add).then_inc(r_kept, 1)

                    e.sem_inc(h_ready, 2)
                    e.sem_inc(lo_ready, 1)
                    e.sem_inc(r_kept, 1)
                    over_groups(e, head, tail)
                    e.wait_ge(tables_in, 96)
                    e.tensor_tensor(relf, rel[:, :, :],
                                    baseb.rearrange("p (s o) -> p s o", o=1).to_broadcast((P, SLOTS, CT)),
                                    ALU.subtract).then_inc(setup, 1)
                    e.wait_ge(consts_in, 32)
                    e.tensor_scalar(base_p[:, :], baseb, k("pmod"), None, ALU.add).then_inc(setup, 1)
                    real = slice(FRONT, FRONT + CHUNKS)
                    e.tensor_tensor(cur, nxt.bitcast(I32), cur.bitcast(I32), ALU.subtract).then_inc(flags, 1)
                    e.tensor_tensor(span, lastb[:, real], baseb[:, real], ALU.subtract).then_inc(flags, 1)
                    e.wait_ge(flags, 2)
                    ahead = lastb[:, FRONT:FRONT + CHUNKS - REACH]
                    e.tensor_tensor(ahead.bitcast(F32), baseb[:, FRONT + REACH:FRONT + CHUNKS], ahead,
                                    ALU.subtract).then_inc(flags, 1)
                    e.tensor_reduce(vm[:, 0:1], cur, AX.X, ALU.min).then_inc(flags, 1)
                    e.tensor_reduce(vm[:, 1:2], span, AX.X, ALU.max).then_inc(flags, 1)
                    e.wait_ge(flags, 5)
                    e.tensor_reduce(vm[:, 2:3], ahead.bitcast(F32), AX.X, ALU.min).then_inc(flags, 1)
                    e.wait_ge(flags, 6)
                    e.tensor_scalar(vf[:, 0:1], vm[:, 0:1], 0.0, None, ALU.is_lt).then_inc(viol_ready, 1)
                    e.tensor_scalar(vf[:, 1:2], vm[:, 1:2], float(W), None, ALU.is_ge).then_inc(viol_ready, 1)
                    e.tensor_scalar(vf[:, 2:3], vm[:, 2:3], 1.0, None, ALU.is_lt).then_inc(viol_ready, 1)
                    e.wait_ge(wt_ready, 1)
                    e.tensor_copy(wt[:, :], pW[:, 0:2 * D]).then_inc(setup, 1)
                    e.tensor_copy(wlg[:, :], pW[:, 2 * D:3 * D]).then_inc(setup, 1)
                    e.wait_ge(r_ready, GROUPS + 1)
                    e.wait_ge(setup, 4)
                    e.memset(temp[:, 0:NW // 2], 0.0).then_inc(setup, 1)
                    e.wait_ge(viol_sum, 1)
                    e.tensor_reduce(fl[:, :], pV[0:1, 0:3], AX.X, ALU.add).then_inc(flags, 1)
                    e.wait_ge(flags, 7)
                    e.tensor_copy(flag[:, 0:1], fl[:, :]).then_inc(setup, 1)
                    e.wait_ge(setup, 6)

                @block.scalar
                def _(e):
                    def scale(t, u):
                        e.wait_ge(stats_ready, t * 2 + (u + 1))
                        e.activation(sd[:, :], mv[:, :, 1], ACT.Sqrt, bias=k("eps")).then_inc(std_ready, 1)

                    def head(t, u):
                        e.wait_ge(scale_ready, t * 2 + (u + 1))
                        e.wait_ge(hT_ready, t * 2 + (u + 1))
                        for j in range(GT):
                            ins = e.activation(hb[:, j, :], xb[:, u, j, :], ACT.Relu,
                                               bias=nb[:, j:j + 1], scale=rs[:, j:j + 1])
                        ins.then_inc(h_ready, 1)

                    def parts(t, u, next_scale):
                        if next_scale is not None:
                            scale(*next_scale)
                        e.wait_ge(stored, t * 2 + (u + 1))
                        e.wait_ge(h_ready, t * 2 + (u + 3))
                        e.activation(hp[:, u, :, 0:D], hb[:, :, :], ACT.Copy).then_inc(hi_ready, 1)
                        e.wait_ge(rest_ready, t * 2 + (u + 1))
                        e.activation(hp[:, u, :, D:2 * D], hr[:, :, :], ACT.Copy).then_inc(mid_ready, 1)

                    def tail(t, u):
                        e.wait_ge(rg_ready, t * 2 + (u + 2))
                        e.wait_ge(stored, t * 2 + (u + 2))
                        e.activation(rgb[:, :, :], pN[:, 0:GC].rearrange("p (t d) -> p t d", d=D), ACT.Copy)\
                            .then_inc(rg_copied, 1)

                    e.wait_ge(consts_in, 32)
                    scale(0, 0)
                    head(0, 0)
                    with e.Fori(0, T0 - 1) as t:
                        for u in range(2):
                            parts(t, u, (t + u, 1 - u))
                            head(t + u, 1 - u)
                            tail(t, u)
                    parts(T0 - 1, 0, (T0 - 1, 1))
                    head(T0 - 1, 1)
                    tail(T0 - 1, 0)
                    parts(T0 - 1, 1, None)
                    tail(T0 - 1, 1)

                @block.tensor
                def _(e):
                    e.sem_inc(r_ready, 1)
                    e.sem_inc(hT_ready, 1)
                    e.wait_ge(consts_in, 32)
                    e.matmul(pW[:, D:2 * D], o("AT"), k("ident"), start=True, stop=False)
                    e.matmul(pW[:, D:2 * D], o("CT"), k("ident"), start=False, stop=True)
                    e.matmul(pW[:, 0:D], o("AT"), o("W_g2"), start=True, stop=False)
                    e.matmul(pW[:, 0:D], o("CT"), o("W_g2"), start=False, stop=False)
                    e.matmul(pW[:, 0:D], o("BT"), o("W_g3"), start=False, stop=False)
                    e.matmul(pW[:, 0:D], o("e_one"), o("b_gate"), start=False, stop=True)
                    e.matmul(pW[:, 2 * D:3 * D], o("W_lT"), k("W_g1"), start=True, stop=True)\
                        .then_inc(wt_ready, 1)

                    def group(t, u):
                        e.wait_ge(h_ready, t * 2 + (u + 3))
                        e.wait_ge(hT_copied, t * 2 + (u + 1))
                        for j in range(GT):
                            ins = e.transpose(pT[:, j * P:(j + 1) * P], hb[:, j, :], k("ident"))
                        ins.then_inc(hT_ready, 1)
                        e.wait_ge(hT_copied, t * 2 + (u + 2))
                        e.wait_ge(r_kept, t * 2 + (u + 1))
                        for b in range(2):
                            ins = e.matmul(pR[:, b * 512:b * 512 + HALF], o("W_r"),
                                           hT[:, b * HALF:(b + 1) * HALF], start=True, stop=True)
                        ins.then_inc(r_ready, 1)
                        e.wait_ge(rT_ready, t * 2 + (u + 1))
                        e.wait_ge(rg_copied, t * 2 + (u + 1))
                        for j in range(GT):
                            ins = e.matmul(pN[:, j * P:(j + 1) * P], rT[:, j * P:(j + 1) * P], k("W_g1"),
                                           start=True, stop=True)
                        ins.then_inc(rg_ready, 1)

                    e.sem_inc(hT_copied, 1)
                    e.sem_inc(rg_copied, 1)
                    e.sem_inc(rg_ready, 1)
                    with e.Fori(0, T0) as t:
                        for u in range(2):
                            group(t, u)
                    e.wait_ge(viol_ready, 3)
                    e.matmul(pV[:, 0:3], k("ones"), vf[:, :], start=True, stop=True).then_inc(viol_sum, 1)

        with ExitStack() as c1:
            g = sb("g", [P, U, CT, 3 * D], BF16, ctx=c1)
            ix = sb("ix", [P, 2, 2 * CT], I32, ctx=c1)
            oh1 = sb("oh1", [P, 2, CT, W], BF16, ctx=c1)
            oh2 = sb("oh2", [P, 2, CT, W], ctx=c1)
            fs = sb("fs", [P, U, EC], ctx=c1)
            e4 = sb("e4", [P, EC], ctx=c1)
            onesb = sb("onesb", [P, P], BF16, ctx=c1)
            rw = sb("rw", [P, 2, 2, D], ctx=c1)
            ag = sb("ag", [P, 2, P], ctx=c1)
            rc = sb("rc", [P, 2], ctx=c1)
            gm = sb("gm", [P, 2, CT, D], ctx=c1)
            pF = ps("pF", [P, 2, CT, 2, D], c1)
            pA = ps("pA", [P, 512], c1)
            pE = ps("pE", [P, 512], c1)
            pG = ps("pG", [P, 512], c1)
            pM = ps("pM", [P, 512], c1)

            ix_in = [sem("ix_in0"), sem("ix_in1")]
            g_in = [sem(f"g_in{u}") for u in range(U)]
            fs_in = [sem("fs_in0"), sem("fs_in1")]
            e4_in = sem("e4_in")
            rw_in = [sem("rw_in0"), sem("rw_in1")]
            oh1_ready = sem("oh1_ready")
            sums_ready = sem("sums_ready")
            sums_added = sem("sums_added")
            emb_in = sem("emb_in")
            emb_ready = sem("emb_ready")
            ag_ready = sem("ag_ready")
            gw_in = sem("gw_in")
            gw_ready = sem("gw_ready")
            ohT_ready = sem("ohT_ready")
            oh2_ready = sem("oh2_ready")
            feat_ready = sem("feat_ready")
            gate_ready = sem("gate_ready")
            msg_ready = sem("msg_ready")
            gsum_ready = sem("gsum_ready")
            gsum_added = sem("gsum_added")
            chain1 = sem("chain1")
            cleared = sem("cleared")
            CLEARS = 5
            TURNS = STEPS // U

            def slot(t, u, shift):
                return t * U + (u + FRONT + shift)

            def load_ix(e, h, t):
                e.dma_start(ix[:, h, :], src[:, bass.ds(t * (U * CT) + 2 * h * CT, 2 * CT)])\
                    .then_inc(ix_in[h], 16)

            def load_bases(e, s, n):
                return nc.values_load_multi_w_load_instructions(
                    base_i[0:1, bass.ds(s, n)], engines=[e.engine], min_val=0, max_val=NW - W)[1]

            with nc.Block() as block:
                @block.sync
                def _(e):
                    with e.If(takes_fast_path(e)):
                        load_ix(e, 0, 0)
                        e.dma_start(e4[:, :], ea4[:, 0, :]).then_inc(e4_in, 16)
                        e.wait_ge(cleared, CLEARS)
                        with e.Fori(0, TURNS) as t:
                            for h in range(2):
                                s0 = slot(t, 2 * h, 1 - LAG)
                                e.wait_ge(gw_ready, t * U + (2 * h + 2))
                                for v, first in enumerate(load_bases(e, slot(t, 2 * h, 1 - LAG), 2)):
                                    e.dma_start(rw[64:64 + W, h, v, :], rg_dram[bass.ds(first, W), :])\
                                        .then_inc(rw_in[h], 16)
                                e.wait_ge(feat_ready, t * U + (2 * h + 3))
                                e.dma_start(fs[0:EA, 2 * h:2 * h + 2, :], ea[:, bass.ds(s0, 2), :])\
                                    .then_inc(fs_in[h], 16)
                                e.dma_start(fs[64:64 + W, 2 * h:2 * h + 2, :].bitcast(I32),
                                            dst_row[0:1, bass.ds(s0, 2), :].to_broadcast((W, 2, EC)))\
                                    .then_inc(fs_in[h], 16)
                                if h == 1:
                                    e.wait_ge(emb_in, t + 1)
                                    e.dma_start(e4[:, :], ea4[:, bass.ds(t + 1, 1), :]
                                                .rearrange("p o c -> p (o c)")).then_inc(e4_in, 16)
                                e.wait_ge(sums_ready, t * U + (U + 2 * h))
                                load_ix(e, 1 - h, t + h)
                        e.wait_ge(ix_in[0], 16 * TURNS + 16)
                        e.wait_ge(ix_in[1], 16 * TURNS)
                        e.wait_ge(e4_in, 16 * TURNS + 16)

                @block.gpsimd
                def _(e):
                    with e.If(takes_fast_path(e)):
                        with e.Fori(0, TURNS) as t:
                            for u in range(U):
                                if u % 2 == 0:
                                    wait_alone(e, ix_in[u // 2], t * 16 + 16, passed)
                                wait_alone(e, sums_ready, t * U + (u + 1), passed)
                                for j in range(CT):
                                    c = (u % 2) * CT + j
                                    e.indirect_dma_start(
                                        g[:, u, j, :], None, h_dram,
                                        bass.IndirectOffsetOnAxis(ap=ix[:, u // 2, c:c + 1], axis=0)
                                    ).then_inc(g_in[u], 16)

                @block.tensor
                def _(e):
                    with e.If(takes_fast_path(e)):
                        e.sem_inc(sums_ready, U)
                        e.sem_inc(feat_ready, U)
                        e.sem_inc(gsum_ready, 1)
                        e.sem_inc(gw_in, 1)
                        e.wait_ge(cleared, CLEARS)
                        with e.Fori(0, TURNS) as t:
                            for u in range(U):
                                b = u % 2
                                e.wait_ge(oh1_ready, t * U + (u + 1))
                                e.wait_ge(sums_added, t * U + (u + 1))
                                e.wait_ge(g_in[u], t * (16 * CT) + 16 * CT)
                                for j in range(CT):
                                    for part in range(3):
                                        e.matmul(pA[:, 0:W], g[:, u, j, part * D:(part + 1) * D], oh1[:, b, j, :],
                                                 start=(j == 0 and part == 0), stop=(j == CT - 1 and part == 2))
                                for j in range(CT):
                                    ins = e.matmul(pA[:, W:2 * W], onesb[:, :], oh1[:, b, j, :],
                                                   start=(j == 0), stop=(j == CT - 1))
                                ins.then_inc(sums_ready, 1)
                                e.wait_ge(emb_ready, t * U + (u + 1))
                                e.wait_ge(gw_ready, t * U + (u + U))
                                e.wait_ge(ohT_ready, t * U + (u + 1))
                                for j in range(CT):
                                    ins = e.matmul(pF[:, b, j, :, :].rearrange("p a d -> p (a d)"),
                                                   fs[:, (u - 1) % U, j * P:(j + 1) * P], wt[:, :],
                                                   start=True, stop=True)
                                ins.then_inc(feat_ready, 1)
                                if u == 0:
                                    wait_alone(e, e4_in, t * 16 + 16, passed)
                                    e.matmul(pE[:, :], k("emb"), e4[:, :], start=True, stop=True)\
                                        .then_inc(emb_in, 1)
                                e.wait_ge(ag_ready, t * U + (u + 1))
                                e.matmul(pG[:, 0:D], ag[:, 0, :], wlg[:, :], start=True, stop=True)
                                e.matmul(pG[:, D:D + 1], ag[0:1, 1, :], k("ones", 1)[:, 0:1],
                                         start=True, stop=True).then_inc(gw_in, 1)
                                e.wait_ge(msg_ready, t * U + (u + 1))
                                e.wait_ge(oh2_ready, t * U + (u + 1))
                                e.wait_ge(gsum_added, t * U + (u + 1))
                                for j in range(CT):
                                    ins = e.matmul(pM[:, 0:W],
                                                   gm[:, 1 - b, j, :], oh2[:, 1 - b, j, :],
                                                   start=(j == 0), stop=(j == CT - 1))
                                ins.then_inc(gsum_ready, 1)

                @block.scalar
                def _(e):
                    with e.If(takes_fast_path(e)):
                        e.wait_ge(cleared, CLEARS)
                        e.sem_inc(emb_ready, 1)

                        def window_sums(first):
                            e.activation(ag[:, :, W:2 * W], ac[:, :, bass.ds(first, W)], ACT.Copy)\
                                .then_inc(ag_ready, 1)

                        window_sums(load_bases(e, FRONT + 1 - LAG, 1)[0])
                        with e.Fori(0, TURNS) as t:
                            for u in range(U):
                                b, h = u % 2, u // 2
                                e.wait_ge(feat_ready, t * U + (u + U + 1))
                                e.wait_ge(gsum_ready, t * U + (u + 1))
                                e.activation(gm[:, b, :, :], pF[:, b, :, 0, :], ACT.Sigmoid).then_inc(gate_ready, 1)
                                e.wait_ge(emb_in, t + 1)
                                e.wait_ge(fs_in[h], t * 32 + 32)
                                e.activation(fs[EA:ONE, u, :], pE[EA * u:EA * u + EE, :], ACT.Relu,
                                             bias=k("b_emb")[EA * u:EA * u + EE, :]).then_inc(emb_ready, 1)
                                if u == 0:
                                    w_next = load_bases(e, slot(t, 1, 1 - LAG), U)
                                e.wait_ge(sums_added, t * U + (u + 2))
                                e.wait_ge(gw_in, t * U + (u + 2))
                                window_sums(w_next[u])

                @block.vector
                def _(e):
                    with e.If(takes_fast_path(e)):
                        e.memset(fs[:, :, :], 1.0).then_inc(cleared, 1)
                        e.memset(onesb[:, :], 1.0).then_inc(cleared, 1)
                        e.memset(ag[:, :, :], 0.0).then_inc(cleared, 1)
                        e.memset(gm[:, :, :, :], 0.0).then_inc(cleared, 1)
                        e.memset(oh2[:, :, :, :], 0.0).then_inc(cleared, 1)
                        e.wait_ge(cleared, CLEARS)
                        e.sem_inc(sums_added, 1)
                        e.sem_inc(gsum_added, 1)
                        e.sem_inc(ohT_ready, 1)
                        e.sem_inc(gw_ready, U)
                        e.sem_inc(msg_ready, 1)
                        e.sem_inc(oh2_ready, 1)

                        def one_hot(to, s):
                            return e.tensor_tensor(
                                to, relf[:, bass.ds(s, 1), :].rearrange("p s (c o) -> p (s c) o", o=1)
                                .to_broadcast((P, CT, W)),
                                k("iota").rearrange("p (o w) -> p o w", o=1).to_broadcast((P, CT, W)),
                                ALU.is_equal)

                        one_hot(oh1[:, 0, :, :], FRONT).then_inc(oh1_ready, 1)
                        with e.Fori(0, TURNS) as t:
                            ch = Chain(e, chain1, t, 2 * U, passed)
                            for u in range(U):
                                b, h, v = u % 2, u // 2, u % 2
                                e.wait_ge(gsum_ready, t * U + (u + 1))
                                one_hot(oh2[:, b, :, :], slot(t, u, -LAG)).then_inc(oh2_ready, 1)
                                wk = load_bases(e, slot(t, u, 0), 1)[0]
                                e.wait_ge(sums_ready, t * U + (u + U + 1))
                                e.wait_ge(sums_added, t * U + (u + 1))
                                e.wait_ge(ag_ready, t * U + (u + 1))
                                to = ac[:, :, bass.ds(wk, W)]
                                e.tensor_tensor(to, to, pA[:, 0:2 * W].rearrange("p (a w) -> p a w", a=2),
                                                ALU.add).then_inc(sums_added, 1)
                                one_hot(oh1[:, 1 - b, :, :], slot(t, u, 1)).then_inc(oh1_ready, 1)
                                wg = load_bases(e, slot(t, u, -1 - LAG), 1)[0]
                                e.wait_ge(gw_in, t * U + (u + 2))
                                ch.then(e.tensor_scalar(rc[64:P, 0:1], pG[64:P, D:D + 1], 1.0, None, ALU.max))
                                ch.wait()
                                ch.then(e.reciprocal(rc[64:P, 1:2], rc[64:P, 0:1]))
                                e.wait_ge(rw_in[h], t * 32 + 32)
                                ch.wait()
                                e.scalar_tensor_tensor(out=wt[64:P, 0:D], in0=pG[64:P, 0:D], scalar=rc[64:P, 1:2],
                                                       in1=rw[64:P, h, v, :], op0=ALU.mult, op1=ALU.add)\
                                    .then_inc(gw_ready, 1)
                                e.wait_ge(fs_in[h], t * 32 + 32)
                                e.tensor_scalar(fs[64:64 + W, u, :], fs[64:64 + W, u, :].bitcast(I32),
                                                base_p[64:64 + W, bass.ds(slot(t, u, 1 - LAG), 1)], None,
                                                ALU.is_equal).then_inc(ohT_ready, 1)
                                e.wait_ge(gate_ready, t * U + (u + 1))
                                e.tensor_tensor(gm[:, b, :, :], gm[:, b, :, :], pF[:, b, :, 1, :],
                                                ALU.mult).then_inc(msg_ready, 1)
                                e.wait_ge(gsum_ready, t * U + (u + 2))
                                e.wait_ge(gsum_added, t * U + (u + 1))
                                to = gs[:, bass.ds(wg, W)]
                                e.tensor_tensor(to, to, pM[:, 0:W], ALU.add).then_inc(gsum_added, 1)
                            ch.close()

        general_pass("sum")

        with ExitStack() as c2:
            ct = sb("ct", [NT, P], ctx=c2)
            cm = sb("cm", [NT, P], ctx=c2)
            sh = sb("sh", [NT, P], ctx=c2)
            dg = sb("dg", [NT, P], ctx=c2)
            nm = sb("nm", [NT, P], ctx=c2)
            sc = sb("sc", [P, 2, GC], ctx=c2)
            mb = sb("mb", [P, 2, GC], ctx=c2)
            pL = ps("pL", [P, 2, 1024], c2)
            pD = ps("pD", [P, 512], c2)
            counts_moved, shares_out, norm_in = sem("counts_moved"), sem("shares_out"), sem("norm_in")
            count_ready, share_ready, deg_ready, norm_ready, norm_turned = (
                sem("count_ready"), sem("share_ready"), sem("deg_ready"), sem("norm_ready"),
                sem("norm_turned"))
            sc_in = [sem("sc_in0"), sem("sc_in1")]
            means_ready = sem("means_ready")
            lin2_ready = sem("lin2_ready")
            group_done = sem("group_done")
            with nc.Block() as block:
                @block.sync
                def _(e):
                    e.dma_start(count_dram.rearrange("(o t) p -> o (t p)", o=1), ac[0:1, 1, 0:NP])\
                        .then_inc(counts_moved, 16)
                    e.wait_ge(counts_moved, 16)
                    e.dma_start(ct[:, :], count_dram).then_inc(counts_moved, 16)
                    e.wait_ge(share_ready, 1)
                    e.dma_start(share_dram, sh[:, :]).then_inc(shares_out, 16)
                    e.wait_ge(norm_ready, 1)
                    e.dma_start(norm_dram, nm[:, :]).then_inc(shares_out, 16)
                    e.wait_ge(shares_out, 32)
                    shares = share_dram.rearrange("(o t) p -> o (t p)", o=1)
                    with e.Fori(0, GROUPS // 2) as t:
                        for u in range(2):
                            e.wait_ge(means_ready, t * 2 + (u + 1))
                            e.dma_start(sc[:, u, :], shares[:, bass.ds((t * 2 + u) * GC, GC)].to_broadcast((P, GC)))\
                                .then_inc(sc_in[u], 16)
                    e.wait_ge(means_ready, GROUPS + 2)
                    e.dma_start(ac[0:HID, 1, 0:NP], norm_dram.rearrange("(o t) p -> o (t p)", o=1)
                                .to_broadcast((HID, NP))).then_inc(norm_in, 16)
                    e.wait_ge(norm_in, 16)

                @block.scalar
                def _(e):
                    e.wait_ge(counts_moved, 32)
                    e.activation(dg[:, :], ct[:, :], ACT.Sqrt, bias=k("ones", NT)[:, 0:1]).then_inc(deg_ready, 1)

                @block.tensor
                def _(e):
                    e.wait_ge(norm_ready, 1)
                    e.transpose(pD[:, 0:NT], nm[:, :], k("ident", NT)[:, 0:NT]).then_inc(norm_turned, 1)
                    with e.Fori(0, GROUPS // 2) as t:
                        for u in range(2):
                            e.wait_ge(means_ready, t * 2 + (u + 3))
                            e.wait_ge(group_done, t * 2 + (u + 1))
                            for b in range(2):
                                ins = e.matmul(pL[:, u, b * 512:b * 512 + HALF], k("W_l"),
                                               mb[:, u, b * HALF:(b + 1) * HALF], start=True, stop=True)
                            ins.then_inc(lin2_ready, 1)

                @block.vector
                def _(e):
                    def means(t, u):
                        wait_alone(e, sc_in[u], t * 16 + 16, passed)
                        e.wait_ge(lin2_ready, t * 2 + (u + 1))
                        e.tensor_tensor(mb[:, u, :], ac[:, 0, bass.ds((t * 2 + u) * GC, GC)], sc[:, u, :],
                                        ALU.mult).then_inc(means_ready, 1)

                    def add(t, u):
                        e.wait_ge(lin2_ready, t * 2 + (u + 3))
                        to = gs[:, bass.ds((t * 2 + u) * GC, GC)].rearrange("p (a b) -> p a b", a=2)
                        e.tensor_tensor(to, to,
                                        pL[:, u, :].rearrange("p (a b) -> p a b", a=2)[:, :, 0:HALF],
                                        ALU.add).then_inc(group_done, 1)

                    e.sem_inc(group_done, 2)
                    e.sem_inc(means_ready, 2)
                    e.sem_inc(lin2_ready, 2)
                    e.wait_ge(counts_moved, 32)
                    e.tensor_scalar(cm[:, :], ct[:, :], 1.0, None, ALU.max).then_inc(count_ready, 1)
                    e.wait_ge(count_ready, 1)
                    e.reciprocal(sh[:, :], cm[:, :]).then_inc(share_ready, 1)
                    e.wait_ge(deg_ready, 1)
                    e.reciprocal(nm[:, :], dg[:, :]).then_inc(norm_ready, 1)
                    e.wait_ge(norm_turned, 1)
                    e.tensor_copy(norm[:, :], pD[:, 0:NT]).then_inc(count_ready, 1)
                    means(0, 0)
                    with e.Fori(0, GROUPS // 2 - 1) as t:
                        for u in range(2):
                            means(t + u, 1 - u)
                            add(t, u)
                    means(GROUPS // 2 - 1, 1)
                    add(GROUPS // 2 - 1, 0)
                    add(GROUPS // 2 - 1, 1)
                    e.wait_ge(group_done, GROUPS + 2)
                    e.wait_ge(count_ready, 2)

        general_pass("gate")

        with ExitStack() as c2:
            bs = sb("bs", [P, N // BN_PIECE, 6], ctx=c2)
            bn_std = sem("bn_std")
            bn_chain = sem("bn_chain")
            with nc.Block() as block:
                @block.scalar
                def _(e):
                    e.wait_ge(bn_chain, 2)
                    e.activation(bn[:, 7:8], bn[:, 1:2], ACT.Sqrt, bias=k("eps")).then_inc(bn_std, 1)

                @block.vector
                def _(e):
                    for i in range(N // BN_PIECE):
                        ins = e.bn_stats(bs[:, i, :], gs[:, i * BN_PIECE:(i + 1) * BN_PIECE])
                    ins.then_inc(bn_chain, 1)
                    e.wait_ge(bn_chain, 1)
                    e.bn_aggr(bn[:, 0:2], bs[:, :, :]).then_inc(bn_chain, 1)
                    e.wait_ge(bn_std, 1)
                    e.reciprocal(bn[:, 2:3], bn[:, 7:8]).then_inc(bn_chain, 1)
                    e.wait_ge(bn_chain, 3)
                    e.scalar_tensor_tensor(out=bn[:, 3:4], in0=bn[:, 2:3], scalar=2.0, in1=k("gamma"),
                                           op0=ALU.mult, op1=ALU.mult).then_inc(bn_chain, 1)
                    e.tensor_scalar(bn[:, 4:5], k("beta"), 2.0, None, ALU.mult).then_inc(bn_chain, 1)
                    e.wait_ge(bn_chain, 5)
                    e.tensor_tensor(bn[:, 5:6], bn[:, 0:1], bn[:, 3:4], ALU.mult).then_inc(bn_chain, 1)
                    e.wait_ge(bn_chain, 6)
                    e.tensor_tensor(bn[:, 6:7], bn[:, 4:5], bn[:, 5:6], ALU.subtract).then_inc(bn_chain, 1)
                    e.wait_ge(bn_chain, 7)

        x2 = ac[:, 0, 0:NP].rearrange("p (t d) -> p t d", d=D)

        with ExitStack() as c3:
            xb = sb("x3", [P, GT, D], ctx=c3)
            yT = sb("y3", [P, GC], ctx=c3)
            hb = sb("h3", [P, GT, D], ctx=c3)
            hT = sb("hT3", [P, GC], ctx=c3)
            hsb = sb("hs3", [P, GT, HID], ctx=c3)
            st = sb("st3", [P, GT, 6], ctx=c3)
            mv = sb("mv3", [P, GT, 2], ctx=c3)
            sd = sb("sd3", [P, GT], ctx=c3)
            rs = sb("rs3", [P, GT], ctx=c3)
            nb = sb("nb3", [P, GT], ctx=c3)
            pT = ps("pT3", [P, 1024], c3)
            pU = ps("pU3", [P, 1024], c3)
            pH = ps("pH3", [P, 512], c3)
            pS = ps("pS3", [HID, 2, 512], c3)
            x3_in, y3_ready, yT3_ready, x2_ready, stats3_ready, std3_ready, scale3_ready, h3_ready = (
                sem("x3_in"), sem("y3_ready"), sem("yT3_ready"), sem("x2_ready"), sem("stats3_ready"),
                sem("std3_ready"), sem("scale3_ready"), sem("h3_ready"))
            hT3_ready, hT3_copied, conv_ready, hs_ready, hs_out, hs_free = (
                sem("hT3_ready"), sem("hT3_copied"), sem("conv_ready"), sem("hs_ready"), sem("hs_out"),
                sem("hs_free"))
            chain3 = sem("chain3")
            with nc.Block() as block:
                @block.sync
                def _(e):
                    with e.Fori(0, GROUPS) as g:
                        e.wait_ge(x2_ready, g + 1)
                        e.dma_start(xb[:, :, :], xg[g]).then_inc(x3_in, 16)

                @block.gpsimd
                def _(e):
                    with e.Fori(0, GROUPS) as g:
                        e.wait_ge(hs_ready, g + 2)
                        e.dma_start(hsg[g], hsb[:, :, :]).then_inc(hs_out, 16)
                        e.wait_ge(hs_out, g * 16 + 16)
                        e.sem_inc(hs_free, 1)

                @block.scalar
                def _(e):
                    def root(g):
                        e.wait_ge(stats3_ready, g + 1)
                        e.activation(sd[:, :], mv[:, :, 1], ACT.Sqrt, bias=k("eps")).then_inc(std3_ready, 1)

                    def head(g):
                        e.wait_ge(scale3_ready, g + 1)
                        e.wait_ge(hT3_ready, g + 1)
                        for j in range(GT):
                            ins = e.activation(hb[:, j, :], x2[:, bass.ds(g * GT + j, 1), :]
                                               .rearrange("p o d -> p (o d)"), ACT.Relu,
                                               bias=nb[:, j:j + 1], scale=rs[:, j:j + 1])
                        ins.then_inc(h3_ready, 1)

                    def relu_bn(g):
                        e.wait_ge(yT3_ready, g + 1)
                        e.activation(yT[:, :], gs[:, bass.ds(g * GC, GC)], ACT.Relu, bias=bn[:, 6:7],
                                     scale=bn[:, 3:4]).then_inc(y3_ready, 1)

                    def tail(g):
                        e.wait_ge(hT3_ready, g + 2)
                        e.wait_ge(conv_ready, g + 1)
                        e.activation(hT[:, :], pU[:, 0:GC], ACT.Copy).then_inc(hT3_copied, 1)

                    relu_bn(0)
                    relu_bn(1)
                    root(0)
                    head(0)
                    with e.Fori(0, GROUPS - 2) as g:
                        relu_bn(g + 2)
                        tail(g)
                        root(g + 1)
                        head(g + 1)
                    tail(GROUPS - 2)
                    root(GROUPS - 1)
                    head(GROUPS - 1)
                    tail(GROUPS - 1)

                @block.tensor
                def _(e):
                    def turn_y(g):
                        e.wait_ge(y3_ready, g + 1)
                        e.wait_ge(x2_ready, g + 1)
                        for j in range(GT):
                            ins = e.transpose(pT[:, j * P:(j + 1) * P], yT[:, j * P:(j + 1) * P], k("ident"))
                        ins.then_inc(yT3_ready, 1)

                    def turn_h(g):
                        e.wait_ge(h3_ready, g + 2)
                        e.wait_ge(hT3_copied, g + 1)
                        for j in range(GT):
                            ins = e.transpose(pU[:, j * P:(j + 1) * P], hb[:, j, :], k("ident"))
                        ins.then_inc(hT3_ready, 1)

                    def conv(g):
                        e.wait_ge(hT3_copied, g + 2)
                        e.wait_ge(hs_ready, g + 1)
                        for j in range(GT):
                            e.matmul(pH[:, j * HID:(j + 1) * HID], hT[:, j * P:(j + 1) * P], k("conv"),
                                     start=True, stop=True)
                        for b in range(2):
                            ins = e.matmul(pS[:, b, 0:HALF], k("conv"), hT[:, b * HALF:(b + 1) * HALF],
                                           start=True, stop=True)
                        ins.then_inc(conv_ready, 1)

                    e.sem_inc(yT3_ready, 1)
                    e.sem_inc(hT3_ready, 1)
                    e.sem_inc(conv_ready, 1)
                    e.sem_inc(hT3_copied, 1)
                    turn_y(0)
                    turn_y(1)
                    with e.Fori(0, GROUPS - 2) as g:
                        turn_h(g)
                        turn_y(g + 2)
                        conv(g)
                    for g in (GROUPS - 2, GROUPS - 1):
                        turn_h(g)
                        conv(g)

                @block.vector
                def _(e):
                    def make_x2(g):
                        x2g = x2[:, bass.ds(g * GT, GT), :]
                        e.wait_ge(x3_in, g * 16 + 16)
                        e.wait_ge(yT3_ready, g + 2)
                        e.tensor_tensor(x2g, xb[:, :, :], pT[:, 0:GC].rearrange("p (t d) -> p t d", d=D),
                                        ALU.add).then_inc(x2_ready, 1)

                    def head(g):
                        ch = Chain(e, chain3, g, 3, passed)
                        wait_alone(e, x2_ready, g + 2, passed)
                        for j in range(GT):
                            ins = e.bn_stats(st[:, j, :], x2[:, bass.ds(g * GT + j, 1), :]
                                             .rearrange("p o d -> p (o d)"))
                        ch.then(ins)
                        ch.wait()
                        for j in range(GT):
                            ins = e.bn_aggr(mv[:, j, :], st[:, j, :])
                        ch.then(ins)
                        ch.wait()
                        e.sem_inc(stats3_ready, 1)
                        e.wait_ge(std3_ready, g + 1)
                        e.wait_ge(h3_ready, g + 1)
                        ch.then(e.reciprocal(rs[:, :], sd[:, :]))
                        ch.wait()
                        e.scalar_tensor_tensor(out=nb[:, :], in0=mv[:, :, 0], scalar=-1.0, in1=rs[:, :],
                                               op0=ALU.mult, op1=ALU.mult).then_inc(scale3_ready, 1)
                        ch.close()

                    def tail(g):
                        cols = bass.ds(g * GC, GC)
                        e.wait_ge(conv_ready, g + 2)
                        e.tensor_tensor(gs[0:HID, cols].rearrange("p (a b) -> p a b", a=2), pS[:, :, 0:HALF],
                                        ac[0:HID, 1, cols].rearrange("p (a b) -> p a b", a=2), ALU.mult)
                        e.wait_ge(hs_free, g + 1)
                        e.tensor_tensor(hsb[:, :, :], pH[:, 0:GT * HID].rearrange("p (t f) -> p t f", f=HID),
                                        norm[:, bass.ds(g * GT, GT)].rearrange("p (t o) -> p t o", o=1)
                                        .to_broadcast((P, GT, HID)), ALU.mult).then_inc(hs_ready, 1)

                    e.sem_inc(x2_ready, 1)
                    e.sem_inc(hs_ready, 1)
                    e.sem_inc(hs_free, 1)
                    e.sem_inc(h3_ready, 1)
                    make_x2(0)
                    head(0)
                    make_x2(1)
                    with e.Fori(0, GROUPS - 2) as g:
                        head(g + 1)
                        make_x2(g + 2)
                        tail(g)
                    head(GROUPS - 1)
                    tail(GROUPS - 2)
                    tail(GROUPS - 1)

        with ExitStack() as c4:
            g = sb("g4", [P, U, CT, HID], ctx=c4)
            ix = sb("ix4", [P, 2, 2 * CT], I32, ctx=c4)
            oh = sb("oh4", [P, 2, CT, W], ctx=c4)
            pA = ps("pA4", [HID, 2, 512], c4)
            ix_in = [sem("ix4_in0"), sem("ix4_in1")]
            g_in = [sem(f"g4_in{u}") for u in range(U)]
            oh_ready = sem("oh4_ready")
            sums_ready = sem("sums4_ready")
            sums_added = sem("sums4_added")
            TURNS = CHUNKS // U
            with nc.Block() as block:
                @block.sync
                def _(e):
                    with e.If(takes_fast_path(e)):
                        with e.Fori(0, TURNS) as t:
                            for h in range(2):
                                e.wait_ge(sums_ready, t * U + (2 * h + 2))
                                e.dma_start(ix[:, h, :], src[:, bass.ds(t * (U * CT) + 2 * h * CT, 2 * CT)])\
                                    .then_inc(ix_in[h], 16)

                @block.gpsimd
                def _(e):
                    with e.If(takes_fast_path(e)):
                        with e.Fori(0, TURNS) as t:
                            for u in range(U):
                                if u % 2 == 0:
                                    wait_alone(e, ix_in[u // 2], t * 16 + 16, passed)
                                wait_alone(e, sums_ready, t * U + (u + 1), passed)
                                for j in range(CT):
                                    c = (u % 2) * CT + j
                                    e.indirect_dma_start(
                                        g[:, u, j, :], None, hs_dram,
                                        bass.IndirectOffsetOnAxis(ap=ix[:, u // 2, c:c + 1], axis=0)
                                    ).then_inc(g_in[u], 16)

                @block.tensor
                def _(e):
                    with e.If(takes_fast_path(e)):
                        e.sem_inc(sums_ready, U)
                        with e.Fori(0, TURNS) as t:
                            for u in range(U):
                                e.wait_ge(oh_ready, t * U + (u + 1))
                                e.wait_ge(sums_added, t * U + (u + 1))
                                e.wait_ge(g_in[u], t * (16 * CT) + 16 * CT)
                                for j in range(CT):
                                    ins = e.matmul(pA[:, u % 2, 0:W], g[:, u, j, :], oh[:, u % 2, j, :],
                                                   start=(j == 0), stop=(j == CT - 1))
                                ins.then_inc(sums_ready, 1)

                @block.vector
                def _(e):
                    with e.If(takes_fast_path(e)):
                        e.sem_inc(sums_added, 2)

                        def one_hot(to, s):
                            return e.tensor_tensor(
                                to, relf[:, bass.ds(s, 1), :].rearrange("p s (c o) -> p (s c) o", o=1)
                                .to_broadcast((P, CT, W)),
                                k("iota").rearrange("p (o w) -> p o w", o=1).to_broadcast((P, CT, W)),
                                ALU.is_equal)

                        one_hot(oh[:, 0, :, :], FRONT).then_inc(oh_ready, 1)
                        with e.Fori(0, TURNS) as t:
                            for u in range(U):
                                e.wait_ge(sums_ready, t * U + (u + U))
                                one_hot(oh[:, 1 - u % 2, :, :], t * U + (u + FRONT + 1)).then_inc(oh_ready, 1)
                                wk = e.value_load(base_i[0:1, bass.ds(t * U + (u + FRONT), 1)],
                                                  min_val=0, max_val=NW - W)
                                e.wait_ge(sums_ready, t * U + (u + U + 1))
                                e.wait_ge(sums_added, t * U + (u + 2))
                                to = gs[0:HID, bass.ds(wk, W)]
                                e.tensor_tensor(to, to, pA[:, u % 2, 0:W], ALU.add).then_inc(sums_added, 1)

        general_pass("conv")

        with ExitStack() as c5:
            z = sb("z", [P, 2, GC], ctx=c5)
            ob = sb("ob", [P, 2, GT, D], ctx=c5)
            pZ = ps("pZ", [P, 2, 1024], c5)
            z0_ready = sem("z0_ready")
            z_ready = sem("z_ready")
            y2_ready = sem("y2_ready")
            o_ready = sem("o_ready")
            o_out = [sem("o_out0"), sem("o_out1")]
            o_free = sem("o_free")
            z_one = sem("z_one")
            zf = sb("zf", [HID, 2, GC], ctx=c5)
            with nc.Block() as block:
                @block.sync
                def _(e):
                    e.sem_inc(o_free, 2)
                    with e.Fori(0, GROUPS // 2) as t:
                        for u in range(2):
                            e.wait_ge(o_ready, t * 2 + (u + 3))
                            e.dma_start(og[t * 2 + u], ob[:, u, :, :]).then_inc(o_out[u], 16)
                        for u in range(2):
                            e.wait_ge(o_out[u], t * 16 + 16)
                            e.sem_inc(o_free, 1)
                    e.wait_ge(o_out[0], 16 * (GROUPS // 2))
                    e.wait_ge(o_out[1], 16 * (GROUPS // 2))

                @block.vector
                def _(e):
                    e.memset(z[HID:HID + 32, :, :], 1.0).then_inc(z_one, 1)
                    e.wait_ge(z_one, 1)
                    e.sem_inc(z_ready, 2)
                    e.sem_inc(o_ready, 2)

                    def sums(t, u):
                        cols = bass.ds((t * 2 + u) * GC, GC)
                        e.wait_ge(z_ready, t * 2 + (u + 1))
                        e.tensor_tensor(zf[:, u, :], gs[0:HID, cols], ac[0:HID, 1, cols], ALU.mult)\
                            .then_inc(z0_ready, 1)

                    def result(t, u):
                        e.wait_ge(y2_ready, t * 2 + (u + 3))
                        e.wait_ge(o_free, t * 2 + (u + 1))
                        e.tensor_tensor(ob[:, u, :, :], x2[:, bass.ds((t * 2 + u) * GT, GT), :],
                                        pZ[:, u, 0:GC].rearrange("p (t d) -> p t d", d=D), ALU.add)\
                            .then_inc(o_ready, 1)

                    sums(0, 0)
                    with e.Fori(0, GROUPS // 2 - 1) as t:
                        for u in range(2):
                            sums(t + u, 1 - u)
                            result(t, u)
                    sums(GROUPS // 2 - 1, 1)
                    result(GROUPS // 2 - 1, 0)
                    result(GROUPS // 2 - 1, 1)

                @block.scalar
                def _(e):
                    with e.Fori(0, GROUPS // 2) as t:
                        for u in range(2):
                            e.wait_ge(z0_ready, t * 2 + (u + 1))
                            e.wait_ge(y2_ready, t * 2 + (u + 1))
                            e.activation(z[0:HID, u, :], zf[:, u, :], ACT.Relu, bias=k("b_conv", HID))\
                                .then_inc(z_ready, 1)

                @block.tensor
                def _(e):
                    e.wait_ge(z_one, 1)
                    e.sem_inc(y2_ready, 2)
                    with e.Fori(0, GROUPS // 2) as t:
                        for u in range(2):
                            e.wait_ge(z_ready, t * 2 + (u + 3))
                            e.wait_ge(o_ready, t * 2 + (u + 1))
                            for j in range(GT):
                                ins = e.matmul(pZ[:, u, j * P:(j + 1) * P], z[0:HID + 1, u, j * P:(j + 1) * P],
                                               k("lin", HID + 1), start=True, stop=True)
                            ins.then_inc(y2_ready, 1)


def kernel(x, src, dst, edge_attr_32, L0_gnn_W_emb, L0_gnn_b_emb, L0_gnn_W_temb, L0_gnn_b_temb,
           L0_gnn_W_tattr, L0_gnn_b_tattr, L0_gnn_W_gate, L0_gnn_b_gate, L0_gnn_W_l, L0_gnn_b_l,
           L0_gnn_W_r, L0_gnn_gamma, L0_gnn_beta, L1_gnn_W_conv, L1_gnn_b_conv, L1_gnn_W_lin,
           L1_gnn_b_lin):
    from concourse import bacc
    from concourse.bass_utils import run_bass_kernel_spmd

    f = np.float32
    x = np.asarray(x)
    src_k = np.zeros(((STEPS + U) * EC,), np.int32)
    src_k[0:E] = src
    dst_k = np.full((SLOTS * EC,), N, np.int32)
    dst_k[FRONT * EC:FRONT * EC + E] = dst
    ea_k = np.zeros((SLOTS * EC, EA), f)
    ea_k[FRONT * EC:FRONT * EC + E] = edge_attr_32

    keep = np.zeros((P, KEEP_N), f)
    once = np.zeros((P, ONCE_N), f)

    def put(to, at, name, a, row=0, col=0):
        lo = at[name][0] + col
        a = np.asarray(a)
        to[row:row + a.shape[0], lo:lo + a.shape[1]] = a

    def keeps(*a, **kw):
        put(keep, KEEP_AT, *a, **kw)

    def onces(*a, **kw):
        put(once, ONCE_AT, *a, **kw)

    W_g = np.asarray(L0_gnn_W_gate)
    keeps("W_l", L0_gnn_W_l)
    keeps("W_g1", W_g[0:D])
    keeps("ident", np.eye(P, dtype=f))
    keeps("ones", np.ones((P, P), f))
    keeps("lin", L1_gnn_W_lin)
    keeps("lin", np.asarray(L1_gnn_b_lin)[None, :], row=HID)
    keeps("conv", L1_gnn_W_conv)
    keeps("iota", np.tile(np.arange(W, dtype=f), (P, 1)))
    keeps("b_l", np.asarray(L0_gnn_b_l)[:, None])
    keeps("gamma", np.asarray(L0_gnn_gamma)[:, None])
    keeps("beta", np.asarray(L0_gnn_beta)[:, None])
    keeps("b_conv", np.asarray(L1_gnn_b_conv)[:, None])
    keeps("pmod", (np.arange(P) % W).astype(f)[:, None])
    keeps("spare", (NP + np.arange(P)).astype(f)[:, None])
    keeps("before", np.tri(P, k=-1, dtype=f))
    keeps("eps", np.full((P, 1), EPS, f))
    for c in range(U):
        keeps("emb", L0_gnn_W_emb, row=EA * c, col=EA * c)
        keeps("b_emb", np.asarray(L0_gnn_b_emb)[:, None], row=EA * c)
    onces("AT", np.asarray(L0_gnn_W_tattr).T)
    onces("AT", np.asarray(L0_gnn_W_temb).T, col=EA)
    onces("AT", np.asarray(L0_gnn_b_temb)[:, None], col=ONE)
    onces("BT", np.asarray(L0_gnn_W_tattr).T)
    onces("BT", np.asarray(L0_gnn_b_tattr)[:, None], col=ONE)
    onces("CT", np.asarray(L0_gnn_b_tattr)[:, None], col=ONE)
    onces("e_one", np.ones((1, 1), f), col=ONE)
    onces("W_g2", W_g[D:2 * D])
    onces("W_g3", W_g[2 * D:3 * D])
    onces("W_r", L0_gnn_W_r)
    onces("W_lT", np.asarray(L0_gnn_W_l).T)
    onces("b_gate", np.asarray(L0_gnn_b_gate)[None, :])

    x_p = np.zeros((NP, D), f)
    x_p[0:N] = x
    arrays = {
        "x": x_p,
        "src": np.ascontiguousarray(src_k.reshape(STEPS + U, CT, P).transpose(2, 0, 1).reshape(P, -1)),
        "dst": np.ascontiguousarray(dst_k.reshape(SLOTS, CT, P).transpose(2, 0, 1)),
        "dst_row": dst_k.reshape(1, SLOTS, EC),
        "base": np.ascontiguousarray(dst_k[::EC][None, :]),
        "last": np.ascontiguousarray(dst_k[EC - 1::EC][None, :]),
        "ea": np.ascontiguousarray(ea_k.T).reshape(EA, SLOTS, EC),
        "ea4": np.ascontiguousarray(
            ea_k[(FRONT + 1 - LAG) * EC:(FRONT + 1 - LAG + STEPS + U) * EC].reshape(-1, U, EC, EA)
            .transpose(1, 3, 0, 2).reshape(P, -1, EC)),
        "keep": keep,
        "once": once,
    }
    nc = bacc.Bacc("TRN2", target_bir_lowering=False, num_devices=1)
    args = {n: nc.dram_tensor(n, a.shape, mybir.dt.from_np(a.dtype), kind="ExternalInput").ap()
            for n, a in arrays.items()}
    args["out"] = nc.dram_tensor("out", (NP, D), F32, kind="ExternalOutput").ap()
    gnn_two_layers(nc, **args)
    r = run_bass_kernel_spmd(nc, [arrays], core_ids=[0])
    return r.results[0]["out"][0:N]
```
